# Optimizing a Trainium2 kernel written in Bass

```python
import numpy as np
import jax
import jax.numpy as jnp

def _softmax(x, axis=-1):
    return jax.nn.softmax(x, axis=axis)

def _gelu(x):
    return jax.nn.gelu(x, approximate=True)

def _silu(x):
    return jax.nn.silu(x)

def _sigmoid(x):
    return jax.nn.sigmoid(x)

def _layernorm(x, axis=-1, eps=1e-05):
    m = jnp.mean(x, axis=axis, keepdims=True)
    v = jnp.var(x, axis=axis, keepdims=True)
    return (x - m) / jnp.sqrt(v + eps)

def _scatter_add(tgt, idx, src, axis=0):
    return tgt.at[idx].add(src)

def _segment_sum(src, seg, n):
    return jax.ops.segment_sum(src, seg, n)
kernel_name = 'mk_adaln_d1_jaxref_r8_69dcf3'

def setup_inputs(seed: int=0):
    np.random.seed(seed)
    _w = jnp.asarray

    def _L0_attn_setup():
        import jax, jax.numpy as jnp
        import numpy as np
        B, N, EMBED, HEADS = (1, 256, 128, 16)
        HD = EMBED // HEADS
        BASE = 10000.0
        EPS = 1e-05

        def _rope(t):
            d = t.shape[-1]
            n = t.shape[-2]
            inv_freq = 1.0 / BASE ** (jnp.arange(0, d, 2, dtype=jnp.float32) / d)
            pos = jnp.arange(n, dtype=jnp.float32)
            ang = pos[:, None] * inv_freq[None, :]
            cos = jnp.concatenate([jnp.cos(ang), jnp.cos(ang)], axis=-1)
            sin = jnp.concatenate([jnp.sin(ang), jnp.sin(ang)], axis=-1)
            t1, t2 = (t[..., :d // 2], t[..., d // 2:])
            rot = jnp.concatenate([-t2, t1], axis=-1)
            return t * cos + rot * sin
        key = jax.random.key(seed)
        ks = jax.random.split(key, 7)
        s = EMBED ** (-0.5)
        return {'x': jax.random.normal(ks[0], (B, N, EMBED), dtype=jnp.float32), 'Wq': jax.random.normal(ks[1], (EMBED, EMBED), dtype=jnp.float32) * s, 'Wk': jax.random.normal(ks[2], (EMBED, EMBED), dtype=jnp.float32) * s, 'Wv': jax.random.normal(ks[3], (EMBED, EMBED), dtype=jnp.float32) * s, 'Wo': jax.random.normal(ks[4], (EMBED, EMBED), dtype=jnp.float32) * s, 'Wg1': jax.random.normal(ks[5], (EMBED, HD), dtype=jnp.float32) * s, 'Wg2': jax.random.normal(ks[6], (HD, EMBED), dtype=jnp.float32) * HD ** (-0.5), 'ln_w': jnp.ones((EMBED,), dtype=jnp.float32), 'ln_b': jnp.zeros((EMBED,), dtype=jnp.float32)}
    _L0_attn_in = _L0_attn_setup()

    def _L0_ffn_setup():
        import jax, jax.numpy as jnp
        import numpy as np
        B, N, D, H, E = (4, 128, 128, 16, 8)
        DK = D // H
        HID = 4 * D
        EPS = 1e-05

        def _layernorm(x, w, b):
            m = jnp.mean(x, axis=-1, keepdims=True)
            v = jnp.mean(jnp.square(x - m), axis=-1, keepdims=True)
            return (x - m) * jax.lax.rsqrt(v + EPS) * w + b

        def _msa(x, w_qkv, w_proj):
            b, n, d = x.shape
            qkv = (x @ w_qkv).reshape(b, n, 3, H, DK)
            q = qkv[:, :, 0].transpose(0, 2, 1, 3)
            k = qkv[:, :, 1].transpose(0, 2, 1, 3)
            v = qkv[:, :, 2].transpose(0, 2, 1, 3)
            attn = jnp.einsum('bhnd,bhmd->bhnm', q, k) * (1.0 / np.sqrt(DK))
            attn = jax.nn.softmax(attn, axis=-1)
            y = jnp.einsum('bhnm,bhmd->bhnd', attn, v)
            y = y.transpose(0, 2, 1, 3).reshape(b, n, d)
            return y @ w_proj

        def _moe_mlp(x, gate_w, gate_b, w1, w2):
            b, n, d = x.shape
            xf = x.reshape(b * n, d)
            logits = xf @ gate_w + gate_b
            one_hot = jax.nn.one_hot(jnp.argmax(logits, axis=-1), E, dtype=xf.dtype)
            h = jax.nn.gelu(jnp.einsum('td,edh->teh', xf, w1), approximate=True)
            y = jnp.einsum('teh,ehd->ted', h, w2)
            out = jnp.einsum('te,ted->td', one_hot, y)
            return out.reshape(b, n, d)
        key = jax.random.key(seed)
        ks = jax.random.split(key, 8)
        s = 0.02
        return {'x': jax.random.normal(ks[0], (B, N, D), jnp.float32), 'ln1_w': jnp.ones((D,), jnp.float32), 'ln1_b': jnp.zeros((D,), jnp.float32), 'w_qkv': jax.random.normal(ks[1], (D, 3 * D), jnp.float32) * s, 'w_proj': jax.random.normal(ks[2], (D, D), jnp.float32) * s, 'ln2_w': jnp.ones((D,), jnp.float32), 'ln2_b': jnp.zeros((D,), jnp.float32), 'gate_w': jax.random.normal(ks[3], (D, E), jnp.float32) * s, 'gate_b': jnp.zeros((E,), jnp.float32), 'w1': jax.random.normal(ks[4], (E, D, HID), jnp.float32) * s, 'w2': jax.random.normal(ks[5], (E, HID, D), jnp.float32) * s}
    _L0_ffn_in = _L0_ffn_setup()
    _L0_c = _w((lambda *s: np.random.randn(*s).astype(np.float32) * 0.05)(8, 128))
    _L0_wmod = _w((lambda *s: np.random.randn(*s).astype(np.float32) * 0.05)(128, 6 * 128) * 128 ** (-0.5))
    _d = {'L0_attn_x': _L0_attn_in['x'], 'L0_attn_Wq': _L0_attn_in['Wq'], 'L0_attn_Wk': _L0_attn_in['Wk'], 'L0_attn_Wv': _L0_attn_in['Wv'], 'L0_attn_Wo': _L0_attn_in['Wo'], 'L0_attn_Wg1': _L0_attn_in['Wg1'], 'L0_attn_Wg2': _L0_attn_in['Wg2'], 'L0_attn_ln_w': _L0_attn_in['ln_w'], 'L0_attn_ln_b': _L0_attn_in['ln_b'], 'L0_ffn_ln1_w': _L0_ffn_in['ln1_w'], 'L0_ffn_ln1_b': _L0_ffn_in['ln1_b'], 'L0_ffn_w_qkv': _L0_ffn_in['w_qkv'], 'L0_ffn_w_proj': _L0_ffn_in['w_proj'], 'L0_ffn_ln2_w': _L0_ffn_in['ln2_w'], 'L0_ffn_ln2_b': _L0_ffn_in['ln2_b'], 'L0_ffn_gate_w': _L0_ffn_in['gate_w'], 'L0_ffn_gate_b': _L0_ffn_in['gate_b'], 'L0_ffn_w1': _L0_ffn_in['w1'], 'L0_ffn_w2': _L0_ffn_in['w2'], 'L0_c': _L0_c, 'L0_wmod': _L0_wmod}
    _x0 = _d['L0_attn_x']
    _d['L0_attn_x'] = jax.random.normal(jax.random.fold_in(jax.random.key(seed), 1), (8, 512, 128), dtype=_x0.dtype)
    del _x0
    return _d

def reference(L0_attn_x, L0_attn_Wq, L0_attn_Wk, L0_attn_Wv, L0_attn_Wo, L0_attn_Wg1, L0_attn_Wg2, L0_attn_ln_w, L0_attn_ln_b, L0_ffn_ln1_w, L0_ffn_ln1_b, L0_ffn_w_qkv, L0_ffn_w_proj, L0_ffn_ln2_w, L0_ffn_ln2_b, L0_ffn_gate_w, L0_ffn_gate_b, L0_ffn_w1, L0_ffn_w2, L0_c, L0_wmod):

    def _L0_attn_ref(x, Wq, Wk, Wv, Wo, Wg1, Wg2, ln_w, ln_b):
        import jax, jax.numpy as jnp
        import numpy as np
        B, N, EMBED, HEADS = (1, 256, 128, 16)
        HD = EMBED // HEADS
        BASE = 10000.0
        EPS = 1e-05

        def _rope(t):
            d = t.shape[-1]
            n = t.shape[-2]
            inv_freq = 1.0 / BASE ** (jnp.arange(0, d, 2, dtype=jnp.float32) / d)
            pos = jnp.arange(n, dtype=jnp.float32)
            ang = pos[:, None] * inv_freq[None, :]
            cos = jnp.concatenate([jnp.cos(ang), jnp.cos(ang)], axis=-1)
            sin = jnp.concatenate([jnp.sin(ang), jnp.sin(ang)], axis=-1)
            t1, t2 = (t[..., :d // 2], t[..., d // 2:])
            rot = jnp.concatenate([-t2, t1], axis=-1)
            return t * cos + rot * sin
        b, n, _ = x.shape
        q = jax.nn.silu(x @ Wq)
        k = jax.nn.silu(x @ Wk)
        v = x @ Wv
        split = lambda t: t.reshape(b, n, HEADS, HD).transpose(0, 2, 1, 3)
        q, k, v = (split(q), split(k), split(v))
        q = _rope(q)
        k = _rope(k)
        energy = jnp.einsum('bhnd,bhmd->bhnm', q, k)
        mask = jnp.tril(jnp.ones((n, n), dtype=energy.dtype))
        energy = energy * mask
        out = jnp.einsum('bhnm,bhmd->bhnd', energy, v)
        out = out.transpose(0, 2, 1, 3).reshape(b, n, EMBED)
        gate = jax.nn.sigmoid(x @ Wg1 @ Wg2)
        out = out * gate
        mu = out.mean(axis=-1, keepdims=True)
        var = ((out - mu) ** 2).mean(axis=-1, keepdims=True)
        out = (out - mu) / jnp.sqrt(var + EPS) * ln_w + ln_b
        return out @ Wo

    def _L0_ffn_ref(x, ln1_w, ln1_b, w_qkv, w_proj, ln2_w, ln2_b, gate_w, gate_b, w1, w2):
        import jax, jax.numpy as jnp
        import numpy as np
        B, N, D, H, E = (4, 128, 128, 16, 8)
        DK = D // H
        HID = 4 * D
        EPS = 1e-05

        def _layernorm(x, w, b):
            m = jnp.mean(x, axis=-1, keepdims=True)
            v = jnp.mean(jnp.square(x - m), axis=-1, keepdims=True)
            return (x - m) * jax.lax.rsqrt(v + EPS) * w + b

        def _msa(x, w_qkv, w_proj):
            b, n, d = x.shape
            qkv = (x @ w_qkv).reshape(b, n, 3, H, DK)
            q = qkv[:, :, 0].transpose(0, 2, 1, 3)
            k = qkv[:, :, 1].transpose(0, 2, 1, 3)
            v = qkv[:, :, 2].transpose(0, 2, 1, 3)
            attn = jnp.einsum('bhnd,bhmd->bhnm', q, k) * (1.0 / np.sqrt(DK))
            attn = jax.nn.softmax(attn, axis=-1)
            y = jnp.einsum('bhnm,bhmd->bhnd', attn, v)
            y = y.transpose(0, 2, 1, 3).reshape(b, n, d)
            return y @ w_proj

        def _moe_mlp(x, gate_w, gate_b, w1, w2):
            b, n, d = x.shape
            xf = x.reshape(b * n, d)
            logits = xf @ gate_w + gate_b
            one_hot = jax.nn.one_hot(jnp.argmax(logits, axis=-1), E, dtype=xf.dtype)
            h = jax.nn.gelu(jnp.einsum('td,edh->teh', xf, w1), approximate=True)
            y = jnp.einsum('teh,ehd->ted', h, w2)
            out = jnp.einsum('te,ted->td', one_hot, y)
            return out.reshape(b, n, d)
        x = x + _msa(_layernorm(x, ln1_w, ln1_b), w_qkv, w_proj)
        x = x + _moe_mlp(_layernorm(x, ln2_w, ln2_b), gate_w, gate_b, w1, w2)
        return x
    x = L0_attn_x
    mod = (_silu(L0_c) @ L0_wmod).reshape(L0_c.shape[0], 6, 1, -1)
    sa, ca, ga, sb, cb, gb = (mod[:, 0], mod[:, 1], mod[:, 2], mod[:, 3], mod[:, 4], mod[:, 5])
    ga = (2 * (ga >= 0) - 1) * jnp.maximum(jnp.abs(ga), 0.25)
    gb = (2 * (gb >= 0) - 1) * jnp.maximum(jnp.abs(gb), 0.25)
    h = _layernorm(x, axis=-1) * (1 + ca) + sa
    x = x + ga * _L0_attn_ref(h, L0_attn_Wq, L0_attn_Wk, L0_attn_Wv, L0_attn_Wo, L0_attn_Wg1, L0_attn_Wg2, L0_attn_ln_w, L0_attn_ln_b)
    h = _layernorm(x, axis=-1) * (1 + cb) + sb
    x = x + gb * _L0_ffn_ref(h, L0_ffn_ln1_w, L0_ffn_ln1_b, L0_ffn_w_qkv, L0_ffn_w_proj, L0_ffn_ln2_w, L0_ffn_ln2_b, L0_ffn_gate_w, L0_ffn_gate_b, L0_ffn_w1, L0_ffn_w2)
    return x

_drawn_inputs = setup_inputs


def setup_inputs(seed=0):
    import zlib

    import numpy as np

    out = dict(_drawn_inputs(seed))
    spreads = {'L0_attn_ln_w': (1.0, 0.2),
     'L0_attn_ln_b': (0.0, 0.333),
     'L0_ffn_ln1_w': (1.0, 0.6),
     'L0_ffn_ln1_b': (0.0, 0.8),
     'L0_ffn_ln2_w': (1.0, 0.6),
     'L0_ffn_ln2_b': (0.0, 0.8),
     'L0_ffn_gate_b': (0.0, 0.701)}
    factors = {'L0_ffn_w_qkv': 8.0,
     'L0_ffn_w_proj': 8.0,
     'L0_ffn_gate_w': 4.784,
     'L0_ffn_w1': 4.306,
     'L0_ffn_w2': 4.229}
    for name, (base, spread) in spreads.items():
        noise = np.random.default_rng([zlib.crc32(name.encode()), seed]).standard_normal(out[name].shape)
        drawn = base * np.exp(spread * noise) if base else spread * noise
        out[name] = jnp.asarray(drawn.astype(out[name].dtype))
    for name, factor in factors.items():
        out[name] = (out[name] * factor).astype(out[name].dtype)
    return out
```

```python
from contextlib import ExitStack

import numpy as np

import concourse.bass as bass
from concourse import mybir

F32 = mybir.dt.float32
F32R = mybir.dt.float32r
ALU = mybir.AluOpType
ACT = mybir.ActivationFunctionType
AX = mybir.AxisListType.X

P = 128
HEADS = 16
HD = P // HEADS
E = 8
LN_X, LN_ATTN, LN_X1, LN_H, LN_X2 = range(5)
LNS = 5
STEPS = 73
EPS = 1e-5
HG = 4
HJ = HEADS // HG
QR = 32

TABLE = {}
_at = 0
for _name, _n in (("ident", P), ("causal", P), ("blockdiag", P), ("head_mask", HEADS), ("cos", 4 * HD),
                  ("sin", 4 * HD), ("k_sel", 3), ("q_sel", 3), ("quad_mask", HJ), ("rank", E)):
    TABLE[_name] = (_at, _n)
    _at += _n
TABLE_COLS = _at


def constants(tokens):
    t = np.zeros((P, TABLE_COLS), np.float32)

    def put(name, values):
        a, n = TABLE[name]
        t[:, a:a + n] = np.asarray(values, np.float32).reshape(P, n)

    p = np.arange(P)
    put("ident", np.eye(P))
    put("causal", p[:, None] <= p[None, :])
    put("blockdiag", p[:, None] // HD == p[None, :] // HD)
    put("head_mask", p[:, None] // HD == np.arange(HEADS)[None, :])
    freq = (1.0 / np.float32(10000.0) ** (np.arange(0, HD, 2, dtype=np.float32) / np.float32(HD))).astype(np.float32)
    pos = (np.arange(tokens // P)[None, :, None] * P + p[:, None, None]).astype(np.float32)
    ang = (pos * freq[None, None, :]).astype(np.float32)
    put("cos", 0.5 * np.concatenate([np.cos(ang), np.cos(ang)], -1))
    put("sin", 0.5 * np.concatenate([-np.sin(ang), np.sin(ang)], -1))
    block = p % QR // HD
    put("k_sel", np.stack([np.choose(block, [1, 1, -1, 0]), np.choose(block, [0, 0, 1, 0]),
                           (block == 3) & (p % HD < 2)], -1))
    put("q_sel", np.stack([np.choose(block, [1, -1, 1, 0]), np.choose(block, [0, 1, 0, 0]), 0 * p], -1))
    put("quad_mask", p[:, None] // QR == np.arange(HJ)[None, :])
    put("rank", np.broadcast_to(np.arange(E) - E, (P, E)))
    return t


def build(nc, a, out, scratch):
    B, S, D = a["x"].shape
    NT = S // P
    HID = a["w1"].shape[2]
    HT = HID // P
    NQ = HG * HJ * NT
    SCALE = float(1.0 / np.sqrt(HD))
    assert D == P and S == 512 and HT == 4 and NT == 4

    with ExitStack() as ctx:
        def sb(name, shape, dt=F32):
            return ctx.enter_context(nc.sbuf_tensor(name, shape, dt))

        def sem(name):
            return ctx.enter_context(nc.semaphore(name))

        table = sb("table", [P, TABLE_COLS])

        def const(name):
            s, n = TABLE[name]
            return table[:, s:s + n]

        ident = const("ident")
        attn_w = sb("attn_w", [P, 3 * P])
        gate1_w = sb("gate1_w", [P, HD])
        gate2_w = sb("gate2_w", [HD, P])
        attn_wo = sb("attn_wo", [P, P])
        msa_w = sb("msa_w", [P, 3 * P])
        rep_w = sb("rep_w", [P, 2, HG, HJ, 4, HD])
        proj_w = sb("proj_w", [P, P])
        router_w = sb("router_w", [P, E])
        router_b = sb("router_b", [P, E])
        w1 = sb("w1", [P, E, HID])
        w2 = sb("w2", [P, E, HT, P])
        ln_cols = sb("ln_cols", [P, 6])
        minus_half = sb("minus_half", [P, NT])
        cT = sb("cT", [P, B])
        cth = sb("cth", [P, B])
        mod = sb("mod", [B, 6 * P])
        modt = sb("modt", [B, 6 * P])
        mod_bc = sb("mod_bc", [P, 6, P])
        x = sb("x", [P, NT, P])
        stats = sb("stats", [P, NT, 6])
        moments = sb("moments", [P, 3, NT])
        vareps = sb("vareps", [P, NT])
        rstd = sb("rstd", [P, NT])
        norm = sb("norm", [P, NT, P])
        h = sb("h", [P, NT, P])
        hT = sb("hT", [P, S])
        rot = sb("rot", [P, NT, 2 * P])
        v = sb("v", [P, NT, P])
        g1T = sb("g1T", [HD, S])
        tanh_gate = sb("tanh_gate", [P, NT, P])
        qT = sb("qT", [P, S])
        kT = sb("kT", [P, S])
        exps = sb("exps", [P, 3, HJ, 2, S])
        last_slot = exps[:, 2].rearrange("p b c d -> p (b c d)")
        scores_m = last_slot[:, 0:16 * P].rearrange("p (a h n) -> p a h n", a=2, h=8)
        tanh_qk, silu_qk = (last_slot[:, a:a + 2 * P * NT].rearrange("p (t n) -> p t n", t=NT)
                            for a in (16 * P, 16 * P + 2 * P * NT))
        acc = last_slot[:, 0:NT * P].rearrange("p (t n) -> p t n", t=NT)
        q_blocks = exps[:, :, :, :, :].rearrange("p a b c d -> p (a b c d)")[:, 0:NT * HEADS * P]\
            .rearrange("p (c h n) -> p c h n", c=NT, h=HEADS)
        state = sb("state", [P, 3, P])
        x1 = sb("x1", [P, NT, P])
        vones = sb("vones", [P, NT, HEADS, QR])
        rounded = sb("rounded", [P, 2, S], F32R)
        kq_parts = sb("kq_parts", [P, 2 * HG, S], F32R)
        q_quads = sb("q_quads", [P, HG, HJ, S], F32R)
        negmax = sb("negmax", [P, HG, HJ, NT])
        negmax_hi = sb("negmax_hi", [P, HG, HJ, NT], F32R)
        shift = sb("shift", [P, HG, NT, HJ, 2])
        shiftT = sb("shiftT", [2 * HJ, HG, S], F32R)
        yT = sb("yT", [P, HG, S])
        recip = sb("recip", [P, NT, HEADS])
        logits = sb("logits", [P, NT, E])
        best = sb("best", [P, NT])
        onehot = sb("onehot", [P, NT, E])
        gelu = exps[:, 0:2].rearrange("p a b c d -> p a (b c d)")[:, :, 0:HT * S]\
            .rearrange("p a (t n) -> p a t n", t=HT)
        y_out = sb("y_out", [P, NT, P])

        bank = ctx.enter_context(nc.psum_tensor("bank", [P, 8, S], F32))

        loaded = sem("loaded")
        prepared = sem("prepared")
        silu_c = sem("silu_c")
        mod_mm = sem("mod_mm")
        mod_step = sem("mod_step")
        mod_ready = sem("mod_ready")
        mod_stored = sem("mod_stored")
        x_landed = sem("x_landed")
        mod_landed = sem("mod_landed")
        dve_step = sem("dve_step")
        var_ready = sem("var_ready")
        rstd_ready = sem("rstd_ready")
        norm_ready = sem("norm_ready")
        pool_step = sem("pool_step")
        h_ready = sem("h_ready")
        transposed = sem("transposed")
        hT_ready = sem("hT_ready")
        qkv_mm = sem("qkv_mm")
        tanh_ready = sem("tanh_ready")
        g1_mm = sem("g1_mm")
        g1_ready = sem("g1_ready")
        gate_mm = sem("gate_mm")
        gate_ready = sem("gate_ready")
        v_ready = sem("v_ready")
        rot_ready = sem("rot_ready")
        qk_transposed = sem("qk_transposed")
        kT_ready = sem("kT_ready")
        qT_ready = sem("qT_ready")
        blocks_ready = sem("blocks_ready")
        scores_mm = sem("scores_mm")
        scores_masked = sem("scores_masked")
        attn_mm = sem("attn_mm")
        state_mm = sem("state_mm")
        state_ready = sem("state_ready")
        gated = sem("gated")
        out_mm = sem("out_mm")
        x1_ready = sem("x1_ready")
        x2_ready = sem("x2_ready")
        vproj_mm = sem("vproj_mm")
        qkproj_mm = sem("qkproj_mm")
        rounded_ready = sem("rounded_ready")
        parts_ready = sem("parts_ready")
        quads_ready = sem("quads_ready")
        max_mm = sem("max_mm")
        max_taken = sem("max_taken")
        shift_ready = sem("shift_ready")
        shift_mm = sem("shift_mm")
        shiftT_ready = sem("shiftT_ready")
        shift_landed = sem("shift_landed")
        s2_mm = sem("s2_mm")
        exp_ready = sem("exp_ready")
        pv_mm = sem("pv_mm")
        yT_ready = sem("yT_ready")
        y_transposed = sem("y_transposed")
        y_ready = sem("y_ready")
        logits_mm = sem("logits_mm")
        up_mm = sem("up_mm")
        gelu_ready = sem("gelu_ready")
        down_mm = sem("down_mm")
        picked = sem("picked")
        y_final = sem("y_final")
        stored = sem("stored")

        N_FIRST, N_LOADS = 16, 17
        U = NQ // 2
        LAG_S2 = 16 + 8
        LAG_PV = 12
        block = ctx.enter_context(nc.Block())

        @block.sync
        def _(sp):
            def load(dst, src):
                sp.dma_start(dst, src).then_inc(loaded, 16)

            load(table[:, :], a["table"])
            load(cT[:, :], a["cT"])
            load(w1[:, 0:2, :].rearrange("p e n -> p (e n)")[:, 0:6 * P], a["wmod"])
            for n, name in enumerate(("Wq", "Wk", "Wv")):
                load(attn_w[:, n * P:(n + 1) * P], a[name])
            load(gate1_w[:, :], a["Wg1"])
            load(gate2_w[:, :], a["Wg2"])
            load(attn_wo[:, :], a["Wo"])
            load(msa_w[:, :], a["w_qkv"])
            load(proj_w[:, :], a["w_proj"])
            load(router_w[:, :], a["gate_w"])
            load(router_b[:, :], a["gate_b"].unsqueeze(0).broadcast_to([P, E]))
            load(ln_cols[:, :], a["ln_cols"])
            load(w1[:, 2:E, :], a["w1"][2:E].rearrange("e p n -> p e n"))
            load(w2[:, :, :, :], a["w2"].rearrange("e (t p) n -> p e t n", p=P))
            sp.wait_ge(mod_mm, 1)
            load(w1[:, 0:2, :], a["w1"][0:2].rearrange("e p n -> p e n"))
            sp.wait_ge(mod_ready, 1)
            sp.dma_start(scratch, mod[:, :]).then_inc(mod_stored, 16)
            sp.wait_ge(mod_stored, 16)
            with sp.Fori(0, B) as i:
                sp.wait_ge(x1_ready, i)
                sp.dma_start(x[:, :, :], a["x"][bass.ds(i, 1)].rearrange("a (t p) d -> p (a t) d", p=P))\
                    .then_inc(x_landed, 16)
                sp.wait_ge(y_final, i)
                sp.dma_start(mod_bc[:, :, :], scratch[bass.ds(i, 1)].rearrange("a (m d) -> a m d", d=P)
                             .broadcast_to([P, 6, P])).then_inc(mod_landed, 16)
                for g in range(HG):
                    sp.wait_ge(shiftT_ready, i * HG + g + 1)
                    for j in range(HJ):
                        r = QR * j + 3 * HD
                        sp.dma_start(q_quads[r:r + 2, g, j, :].bitcast(F32), shiftT[2 * j:2 * j + 2, g, :].bitcast(F32))\
                            .then_inc(shift_landed, 16)
                sp.wait_ge(y_final, i + 1)
                sp.dma_start(out[bass.ds(i, 1)].rearrange("a (t p) d -> p (a t) d", p=P), y_out[:, :, :])\
                    .then_inc(stored, 16)
            sp.wait_ge(stored, 16 * B)

        @block.gpsimd
        def _(pool):
            nc.gpsimd.memset(minus_half[:, :], -0.5).then_inc(prepared, 1)
            pool.wait_ge(loaded, 16 * N_LOADS)
            with pool.Fori(0, B) as i:
                def rsqrt(n):
                    pool.wait_ge(var_ready, i * LNS + n + 1)
                    nc.gpsimd.tensor_tensor(rstd[:, :], vareps[:, :], minus_half[:, :], ALU.pow)\
                        .then_inc(rstd_ready, 1)

                def modulate(n, scale, bias):
                    pool.wait_ge(norm_ready, i * LNS + (LN_X, LN_X1)[n] + 1)
                    nc.gpsimd.tensor_tensor(h[:, :, :], norm[:, :, :],
                                            mod_bc[:, scale, :].unsqueeze(1).broadcast_to([P, NT, P]), ALU.mult)\
                        .then_inc(pool_step, 1)
                    pool.wait_ge(pool_step, i * 2 + n + 1)
                    nc.gpsimd.tensor_tensor(h[:, :, :], h[:, :, :],
                                            mod_bc[:, bias, :].unsqueeze(1).broadcast_to([P, NT, P]), ALU.add)\
                        .then_inc(h_ready, 1)

                rsqrt(LN_X)
                modulate(0, 1, 0)
                pool.wait_ge(qT_ready, i + 1)
                for c in range(NT):
                    nc.gpsimd.tensor_tensor(q_blocks[:, c], qT[:, c * P:(c + 1) * P].unsqueeze(1)
                                            .broadcast_to([P, HEADS, P]),
                                            const("head_mask").unsqueeze(2).broadcast_to([P, HEADS, P]), ALU.mult)\
                        .then_inc(blocks_ready, 1)
                rsqrt(LN_ATTN)
                rsqrt(LN_X1)
                modulate(1, 4, 3)
                rsqrt(LN_H)
                for g in range(HG):
                    pool.wait_ge(parts_ready, i * 2 * HG + 2 * g + 2)
                    nc.gpsimd.tensor_tensor(q_quads[:, g], kq_parts[:, 2 * g + 1, :].bitcast(F32).unsqueeze(1)
                                            .broadcast_to([P, HJ, S]),
                                            const("quad_mask").unsqueeze(2).broadcast_to([P, HJ, S]), ALU.mult)\
                        .then_inc(quads_ready, 1)
                rsqrt(LN_X2)

        @block.scalar
        def _(act):
            act.wait_ge(loaded, 16 * N_FIRST)
            nc.scalar.activation(cth[:, :], cT[:, :], ACT.Tanh, scale=0.5).then_inc(silu_c, 1)
            with act.Fori(0, B) as i:
                def copy_T(n, w, b):
                    act.wait_ge(transposed, i * 5 + n + 1)
                    nc.scalar.activation(hT[:, :], bank[:, 7, :], ACT.Identity, scale=w, bias=b)\
                        .then_inc(hT_ready, 1)

                copy_T(0, 1.0, 0.0)
                act.wait_ge(qkv_mm, i + 1)
                nc.scalar.activation(tanh_qk[:, :, :], bank[:, 2:6, 0:2 * P], ACT.Tanh, scale=0.5)\
                    .then_inc(tanh_ready, 1)
                act.wait_ge(gate_mm, i + 1)
                nc.scalar.activation(tanh_gate[:, :, :].rearrange("p t n -> p (t n)"), bank[:, 7, :], ACT.Tanh,
                                     scale=0.5).then_inc(gate_ready, 1)
                act.wait_ge(qk_transposed, i + 1)
                nc.scalar.activation(qT[:, :], bank[:, 0, :], ACT.Identity).then_inc(qT_ready, 1)
                nc.scalar.activation(kT[:, :], bank[:, 1, :], ACT.Identity).then_inc(kT_ready, 1)
                copy_T(1, ln_cols[:, 0:1], ln_cols[:, 1:2])
                copy_T(2, ln_cols[:, 2:3], ln_cols[:, 3:4])
                for r in range(2 * HG):
                    act.wait_ge(qkproj_mm, i * 2 * HG + r + 1)
                    if r >= 2:
                        act.wait_ge(parts_ready, i * 2 * HG + r - 1)
                    s = const(("k_sel", "q_sel")[r % 2])
                    nc.scalar.activation(rounded[:, r % 2, :], bank[:, 2 + r % 4, :], ACT.Identity,
                                         scale=s[:, 0:1], bias=s[:, 2:3]).then_inc(rounded_ready, 1)

                def copy_y(g):
                    act.wait_ge(pv_mm, i * 2 * HG + 2 * g + 2)
                    nc.scalar.activation(yT[:, g, :], bank[:, 6, :], ACT.Identity).then_inc(yT_ready, 1)

                for u in range(U):
                    grp, j = u // HJ, u % HJ
                    act.wait_ge(s2_mm, i * U + u + 1)
                    if j == 0 and grp >= 3:
                        act.wait_ge(pv_mm, i * 2 * HG + grp - 2)
                    nc.scalar.activation(exps[:, grp % 3, j], bank[:, 2 + 2 * (u % 2):4 + 2 * (u % 2), :],
                                         ACT.Exp, scale=SCALE).then_inc(exp_ready, 1)
                    if u >= 12 and u % 8 == 4:
                        copy_y((u - 12) // 8)
                copy_y(HG - 1)
                copy_T(3, 1.0, 0.0)
                copy_T(4, ln_cols[:, 4:5], ln_cols[:, 5:6])
                for r in range(E * HT):
                    e, t = divmod(r, HT)
                    act.wait_ge(up_mm, i * E * HT + r + 1)
                    if t == 0 and e >= 2:
                        act.wait_ge(down_mm, i * E + e - 1)
                    nc.scalar.activation(gelu[:, e % 2, t, :], bank[:, 2 + r % 4, :], ACT.Gelu_apprx_tanh)\
                        .then_inc(gelu_ready, 1)

        @block.tensor
        def _(pe):
            mm = nc.tensor.matmul
            pe.wait_ge(silu_c, 2)
            wmod = w1[:, 0:2, :].rearrange("p e n -> p (e n)")
            mm(bank[0:B, 0, :], cth[:, :], wmod[:, 0:S], start=True, stop=True)
            mm(bank[0:B, 1, 0:2 * P], cth[:, :], wmod[:, S:6 * P], start=True, stop=True).then_inc(mod_mm, 1)
            pe.wait_ge(loaded, 16 * N_LOADS)
            pe.wait_ge(prepared, 12)
            with pe.Fori(0, B) as i:
                def tile(T, t):
                    return T[:, t * P:(t + 1) * P]

                def transpose_tiles(b, src, signal):
                    for t in range(NT):
                        last = nc.tensor.transpose(tile(bank[:, b, :], t), src(t), ident)
                    if signal is not None:
                        last.then_inc(signal, 1)

                pe.wait_ge(h_ready, i * 2 + 1)
                transpose_tiles(7, lambda t: h[:, t, :], transposed)
                pe.wait_ge(hT_ready, i * 5 + 1)
                for t in range(NT):
                    last = mm(bank[:, 2 + t, 0:3 * P], tile(hT, t), attn_w[:, :], start=True, stop=True)
                last.then_inc(qkv_mm, 1)
                mm(bank[0:HD, 6, :], gate1_w[:, :], hT[:, :], start=True, stop=True).then_inc(g1_mm, 1)
                pe.wait_ge(g1_ready, i + 1)
                for t in range(NT):
                    last = mm(tile(bank[:, 7, :], t), tile(g1T, t), gate2_w[:, :], start=True, stop=True)
                last.then_inc(gate_mm, 1)
                pe.wait_ge(rot_ready, i + 1)
                transpose_tiles(0, lambda t: rot[:, t, 0:P], None)
                transpose_tiles(1, lambda t: rot[:, t, P:2 * P], qk_transposed)
                pe.wait_ge(kT_ready, i + 1)

                def scores(u):
                    c, half = divmod(u, 2)
                    if half == 0:
                        pe.wait_ge(blocks_ready, i * NT + c + 1)
                    if u >= 2:
                        pe.wait_ge(scores_masked, i * 2 * NT + u - 1)
                    for n in range(2):
                        hh = 8 * half + 4 * n
                        last = mm(bank[:, 2 + 2 * (u % 2) + n, :], tile(kT, c),
                                  q_blocks[:, c, hh:hh + 4, :].rearrange("p h n -> p (h n)"),
                                  start=True, stop=True)
                    last.then_inc(scores_mm, 1)

                def attend(u):
                    c, half = divmod(u, 2)
                    if half == 0:
                        if c >= 2:
                            pe.wait_ge(gated, i * NT + c - 1)
                        if c >= 1:
                            pe.wait_ge(state_ready, i * (NT - 1) + c)
                            mm(bank[:, c % 2, 0:P], tile(qT, c), state[:, c - 1, :], start=True, stop=False,
                               skip_group_check=True)
                        if c < NT - 1:
                            mm(bank[:, 6, 0:P], rot[:, c, P:2 * P], v[:, c, :], start=True, stop=True)\
                                .then_inc(state_mm, 1)
                    pe.wait_ge(scores_masked, i * 2 * NT + u + 1)
                    for hh in range(8):
                        at = slice((8 * half + hh) * HD, (8 * half + hh + 1) * HD)
                        last = mm(bank[:, c % 2, at], scores_m[:, u % 2, hh, :], v[:, c, at],
                                  start=c == 0, stop=True, skip_group_check=True)
                    last.then_inc(attn_mm, 1)

                scores(0)
                scores(1)
                for u in range(2 * NT):
                    attend(u)
                    if u + 2 < 2 * NT:
                        scores(u + 2)
                pe.wait_ge(norm_ready, i * LNS + LN_ATTN + 1)
                transpose_tiles(7, lambda t: norm[:, t, :], transposed)
                pe.wait_ge(hT_ready, i * 5 + 2)
                for t in range(NT):
                    last = mm(tile(bank[:, 0, :], t), tile(hT, t), attn_wo[:, :], start=True, stop=True)
                last.then_inc(out_mm, 1)

                pe.wait_ge(norm_ready, i * LNS + LN_H + 1)
                transpose_tiles(7, lambda t: norm[:, t, :], transposed)
                pe.wait_ge(hT_ready, i * 5 + 3)
                for t in range(NT):
                    last = mm(tile(bank[:, 6, :], t), tile(hT, t), msa_w[:, 2 * P:3 * P], start=True, stop=True)
                last.then_inc(vproj_mm, 1)
                for r in range(2 * HG):
                    if r >= 4:
                        pe.wait_ge(parts_ready, i * 2 * HG + r - 3)
                    mm(bank[:, 2 + r % 4, :], rep_w[:, 1 - r % 2, r // 2].rearrange("p j c d -> p (j c d)"),
                       hT[:, :], start=True, stop=True).then_inc(qkproj_mm, 1)

                def k_part(g):
                    return kq_parts[:, 2 * g, :]

                def max_scores(a):
                    g, j, t = a // (HJ * NT), a // NT % HJ, a % NT
                    if j == t == 0:
                        pe.wait_ge(quads_ready, i * HG + g + 1)
                    if a >= 2:
                        pe.wait_ge(max_taken, i * NQ + a - 1)
                    mm(bank[:, a % 2, :], tile(q_quads[:, g, j], t), k_part(g), start=True, stop=True)\
                        .then_inc(max_mm, 1)

                def shift_rows(g):
                    pe.wait_ge(shift_ready, i * HG + g + 1)
                    if g >= 1:
                        pe.wait_ge(shiftT_ready, i * HG + g)
                    for t in range(NT):
                        last = mm(tile(bank[0:2 * HJ, 7, :], t), shift[:, g, t].rearrange("p j s -> p (j s)"),
                                  ident, start=True, stop=True)
                    last.then_inc(shift_mm, 1)

                def shifted_scores(m):
                    u, n = divmod(m, 2)
                    g, half, j = u // 8, u // 4 % 2, u % 4
                    if m % 16 == 0:
                        pe.wait_ge(shift_landed, i * 16 * HG * HJ + 16 * HJ * (g + 1))
                    if u >= 2 and n == 0:
                        pe.wait_ge(exp_ready, i * U + u - 1)
                    last = mm(bank[:, 2 + 2 * (u % 2) + n, :], tile(k_part(g), 2 * half + n), q_quads[:, g, j],
                              start=True, stop=True)
                    if n == 1:
                        last.then_inc(s2_mm, 1)

                def weighted_values(n):
                    w, k, j = n // 8, n // 4 % 2, n % 4
                    g, half = divmod(w, 2)
                    if n % 8 == 0:
                        pe.wait_ge(exp_ready, i * U + 4 * (w + 1))
                        if g >= 1 and half == 0:
                            pe.wait_ge(yT_ready, i * HG + g)
                        if n == 0:
                            pe.wait_ge(v_ready, i * 2 + 2)
                    last = mm(bank[QR * j:QR * (j + 1), 6, :], vones[:, 2 * half + k, HJ * g + j, :],
                              exps[:, w % 3, j, k, :], start=half == 0 and k == 0, stop=half == 1 and k == 1)
                    if n % 8 == 7:
                        last.then_inc(pv_mm, 1)

                for s in range(NQ + LAG_S2 + LAG_PV):
                    if s < NQ:
                        max_scores(s)
                    if s % 16 == 2 and 1 <= s // 16 <= HG:
                        shift_rows(s // 16 - 1)
                    if 0 <= s - LAG_S2 < NQ:
                        shifted_scores(s - LAG_S2)
                    if 0 <= s - LAG_S2 - LAG_PV:
                        weighted_values(s - LAG_S2 - LAG_PV)

                pe.wait_ge(yT_ready, i * HG + HG)
                for t in range(NT):
                    for g in range(HG):
                        last = nc.tensor.transpose(tile(bank[:, 2 + t, :], g), tile(yT[:, g], t), ident)
                last.then_inc(y_transposed, 1)
                pe.wait_ge(y_ready, i + 1)
                transpose_tiles(7, lambda t: v[:, t, :], transposed)
                pe.wait_ge(hT_ready, i * 5 + 4)
                for t in range(NT):
                    last = mm(tile(bank[:, 0, :], t), tile(hT, t), proj_w[:, :], start=True, stop=True)
                last.then_inc(out_mm, 1)

                pe.wait_ge(norm_ready, i * LNS + LN_X2 + 1)
                transpose_tiles(7, lambda t: norm[:, t, :], transposed)
                pe.wait_ge(hT_ready, i * 5 + 5)
                for t in range(NT):
                    last = mm(bank[:, 1, t * E:(t + 1) * E], tile(hT, t), router_w[:, :], start=True, stop=True)
                last.then_inc(logits_mm, 1)

                def up(e):
                    for t in range(HT):
                        r = e * HT + t
                        if r >= 4:
                            pe.wait_ge(gelu_ready, i * E * HT + r - 3)
                        mm(bank[:, 2 + r % 4, :], w1[:, e, t * P:(t + 1) * P], hT[:, :], start=True, stop=True)\
                            .then_inc(up_mm, 1)

                def down(e):
                    pe.wait_ge(gelu_ready, i * E * HT + (e + 1) * HT)
                    if e >= 2:
                        pe.wait_ge(picked, i * E + e - 1)
                    for t in range(NT):
                        for n in range(HT):
                            last = mm(tile(bank[:, 6 + e % 2, :], t), tile(gelu[:, e % 2, n], t), w2[:, e, n, :],
                                      start=n == 0, stop=n == HT - 1)
                    last.then_inc(down_mm, 1)

                up(0)
                for e in range(E):
                    if e + 1 < E:
                        up(e + 1)
                    down(e)

        @block.vector
        def _(dve):
            V = nc.vector
            dve.wait_ge(silu_c, 1)
            V.scalar_tensor_tensor(cth[:, :], cth[:, :], 1.0, cT[:, :], ALU.add, ALU.mult).then_inc(silu_c, 1)
            V.memset(rep_w[:, :, :, :, :, :].rearrange("p a b c d e -> p (a b c d e)"), 0.0).then_inc(prepared, 1)
            V.memset(vones[:, :, :, :].rearrange("p a b c -> p (a b c)"), 0.0).then_inc(prepared, 1)
            dve.wait_ge(prepared, 3)
            V.memset(vones[:, :, :, HD:HD + 1].rearrange("p a b c -> p (a b c)"), 1.0).then_inc(prepared, 1)
            for part in range(2):
                for g in range(HG):
                    src = msa_w[:, part * P + g * QR:part * P + (g + 1) * QR].rearrange("p (j d) -> p j d", d=HD)
                    V.tensor_copy(rep_w[:, part, g, :, 0:3, :], src.unsqueeze(2).broadcast_to([P, HJ, 3, HD]))\
                        .then_inc(prepared, 1)
            dve.wait_ge(mod_mm, 1)
            V.tensor_scalar(mod[:, 0:S], bank[0:B, 0, :], 0.5, None, ALU.mult).then_inc(mod_step, 1)
            V.tensor_scalar(mod[:, S:6 * P], bank[0:B, 1, 0:2 * P], 0.5, None, ALU.mult).then_inc(mod_step, 1)
            dve.wait_ge(mod_step, 2)
            for n, m in enumerate((1, 4)):
                V.tensor_scalar(mod[:, m * P:(m + 1) * P], mod[:, m * P:(m + 1) * P], 1.0, None, ALU.add)\
                    .then_inc(mod_step, 1)
            for n, m in enumerate((2, 5)):
                V.tensor_scalar(modt[:, m * P:(m + 1) * P], mod[:, m * P:(m + 1) * P], 0.0, 2.0, ALU.is_ge,
                                ALU.mult).then_inc(mod_step, 1)
            for n, m in enumerate((2, 5)):
                gate = mod[:, m * P:(m + 1) * P]
                dve.wait_ge(mod_step, 6 + 3 * n)
                V.scalar_tensor_tensor(gate, gate, -1.0, gate, ALU.mult, ALU.max).then_inc(mod_step, 1)
                dve.wait_ge(mod_step, 7 + 3 * n)
                V.tensor_scalar(gate, gate, 0.25, None, ALU.max).then_inc(mod_step, 1)
                dve.wait_ge(mod_step, 8 + 3 * n)
                V.scalar_tensor_tensor(gate, modt[:, m * P:(m + 1) * P], -1.0, gate, ALU.add, ALU.mult)\
                    .then_inc(mod_step, 1)
            dve.wait_ge(mod_step, 12)
            V.engine_nop().then_inc(mod_ready, 1)
            dve.wait_ge(prepared, 12)
            with dve.Fori(0, B) as i:
                steps = [0]

                def step(instruction):
                    steps[0] += 1
                    instruction.then_inc(dve_step, 1)

                def settle():
                    dve.wait_ge(dve_step, i * STEPS + steps[0])

                def layer_norm(n, src, eps):
                    for t in range(NT):
                        step(V.bn_stats(stats[:, t, :], src[:, t, :]))
                    settle()
                    (mean_e, var_e), (mean_o, var_o) = ((stats[:, :, n], stats[:, :, n + 1]) for n in (1, 4))
                    mean, diff, var = (moments[:, n, :] for n in range(3))
                    step(V.tensor_tensor(mean, mean_e, mean_o, ALU.add))
                    step(V.tensor_tensor(diff, mean_e, mean_o, ALU.subtract))
                    step(V.tensor_tensor(var, var_e, var_o, ALU.add))
                    settle()
                    step(V.tensor_scalar(mean, mean, 0.5, None, ALU.mult))
                    step(V.tensor_tensor(diff, diff, diff, ALU.mult))
                    step(V.tensor_scalar(var, var, 1.0 / P, eps, ALU.mult, ALU.add))
                    settle()
                    V.scalar_tensor_tensor(vareps[:, :], diff, 0.25, var, ALU.mult, ALU.add).then_inc(var_ready, 1)
                    dve.wait_ge(rstd_ready, i * LNS + n + 1)
                    for t in range(NT):
                        last = V.tensor_scalar(norm[:, t, :], src[:, t, :], mean[:, t:t + 1], rstd[:, t:t + 1],
                                               ALU.subtract, ALU.mult)
                    last.then_inc(norm_ready, 1)

                dve.wait_ge(x_landed, 16 * i + 16)
                dve.wait_ge(mod_landed, 16 * i + 16)
                layer_norm(LN_X, x, EPS)
                dve.wait_ge(g1_mm, i + 1)
                V.tensor_copy(g1T[:, :], bank[0:HD, 6, :]).then_inc(g1_ready, 1)
                dve.wait_ge(tanh_ready, i + 1)
                V.tensor_copy(v[:, :, :], bank[:, 2:6, 2 * P:3 * P]).then_inc(v_ready, 1)
                step(V.scalar_tensor_tensor(silu_qk[:, :, :], tanh_qk[:, :, :], 1.0, bank[:, 2:6, 0:2 * P],
                                            ALU.add, ALU.mult))
                settle()
                heads = silu_qk[:, :, :].rearrange("p t (h d) -> p t h d", d=HD)
                cross = tanh_qk[:, :, :].rearrange("p t (h d) -> p t h d", d=HD)
                hd2 = HD // 2
                cos = const("cos").rearrange("p (t d) -> p t d", d=HD).unsqueeze(2)
                sin = const("sin").rearrange("p (t d) -> p t d", d=HD).unsqueeze(2)
                step(V.tensor_tensor(rot[:, :, :].rearrange("p t (h d) -> p t h d", d=HD), heads,
                                     cos.broadcast_to([P, NT, 2 * HEADS, HD]), ALU.mult))
                for d0, d1 in ((0, hd2), (hd2, 0)):
                    step(V.tensor_tensor(cross[:, :, :, d0:d0 + hd2], heads[:, :, :, d1:d1 + hd2],
                                         sin[:, :, :, d0:d0 + hd2].broadcast_to([P, NT, 2 * HEADS, hd2]), ALU.mult))
                settle()
                V.tensor_tensor(rot[:, :, :], rot[:, :, :], tanh_qk[:, :, :], ALU.add).then_inc(rot_ready, 1)

                def add_state(c):
                    dve.wait_ge(state_mm, i * (NT - 1) + c + 1)
                    masked = V.tensor_tensor(state[:, c, :], bank[:, 6, 0:P], const("blockdiag"), ALU.mult)
                    if c == 0:
                        masked.then_inc(state_ready, 1)
                    else:
                        step(masked)
                        settle()
                        V.tensor_tensor(state[:, c, :], state[:, c, :], state[:, c - 1, :], ALU.add)\
                            .then_inc(state_ready, 1)

                def gate_chunk(c):
                    dve.wait_ge(attn_mm, i * 2 * NT + 2 * c + 2)
                    V.scalar_tensor_tensor(h[:, c, :], tanh_gate[:, c, :], 1.0, bank[:, c % 2, 0:P],
                                           ALU.add, ALU.mult).then_inc(gated, 1)

                dve.wait_ge(gate_ready, i + 1)
                for u in range(2 * NT):
                    dve.wait_ge(scores_mm, i * 2 * NT + u + 1)
                    if u >= 2:
                        dve.wait_ge(attn_mm, i * 2 * NT + u - 1)
                    V.tensor_tensor(scores_m[:, u % 2], bank[:, 2 + 2 * (u % 2):4 + 2 * (u % 2), :]
                                    .rearrange("p b (h n) -> p (b h) n", n=P),
                                    const("causal").unsqueeze(1).broadcast_to([P, 8, P]), ALU.mult)\
                        .then_inc(scores_masked, 1)
                    if u % 2 == 0 and u < 2 * (NT - 1):
                        add_state(u // 2)
                    if u % 2 == 0 and u >= 2:
                        gate_chunk(u // 2 - 1)
                gate_chunk(NT - 1)
                dve.wait_ge(gated, i * NT + NT)
                layer_norm(LN_ATTN, h, 4 * EPS)

                def scaled(n, dst, src, m, plus):
                    step(V.tensor_tensor(dst[:, :, :], src, mod_bc[:, m, :].unsqueeze(1).broadcast_to([P, NT, P]),
                                         ALU.mult))
                    settle()
                    return V.tensor_tensor(dst[:, :, :], dst[:, :, :], plus[:, :, :], ALU.add)

                def tiles(b):
                    return bank[:, b, :].rearrange("p (t n) -> p t n", n=P)

                dve.wait_ge(out_mm, i * 2 + 1)
                scaled(0, x1, tiles(0), 2, x).then_inc(x1_ready, 1)
                dve.wait_ge(x1_ready, i + 1)
                layer_norm(LN_X1, x1, EPS)
                dve.wait_ge(h_ready, i * 2 + 2)
                layer_norm(LN_H, h, EPS)
                dve.wait_ge(vproj_mm, i + 1)
                V.tensor_copy(vones[:, :, :, 0:HD], bank[:, 6, :].rearrange("p (t h d) -> p t h d", h=HEADS, d=HD))\
                    .then_inc(v_ready, 1)
                for r in range(2 * HG):
                    dve.wait_ge(rounded_ready, i * 2 * HG + r + 1)
                    V.scalar_tensor_tensor(kq_parts[:, r, :], bank[:, 2 + r % 4, :],
                                           const(("k_sel", "q_sel")[r % 2])[:, 1:2],
                                           rounded[:, r % 2, :].bitcast(F32), ALU.mult, ALU.add)\
                        .then_inc(parts_ready, 1)

                def split_maxima(g):
                    dve.wait_ge(max_taken, i * NQ + 16 * (g + 1))
                    step(V.tensor_copy(negmax_hi[:, g], negmax[:, g]))
                    settle()
                    hi = negmax_hi[:, g].bitcast(F32).rearrange("p j t -> p t j")
                    step(V.tensor_copy(shift[:, g, :, :, 0], hi))
                    V.tensor_tensor(shift[:, g, :, :, 1], negmax[:, g].rearrange("p j t -> p t j"), hi,
                                    ALU.subtract).then_inc(shift_ready, 1)

                def copy_shift(g):
                    dve.wait_ge(shift_mm, i * HG + g + 1)
                    V.tensor_copy(shiftT[:, g, :], bank[0:2 * HJ, 7, :]).then_inc(shiftT_ready, 1)

                for a in range(NQ):
                    g, j, t = a // (HJ * NT), a // NT % HJ, a % NT
                    dve.wait_ge(max_mm, i * NQ + a + 1)
                    V.tensor_reduce(negmax[:, g, j, t:t + 1], bank[:, a % 2, :], AX, ALU.max, negate=True)\
                        .then_inc(max_taken, 1)
                    if a % 16 == 15:
                        split_maxima(g)
                    if a % 16 == 2 and g >= 1:
                        copy_shift(g - 1)
                copy_shift(HG - 1)
                dve.wait_ge(y_transposed, i + 1)
                sums = bank[:, 2:6, :].rearrange("p t (h r) -> p t h r", r=QR)
                step(V.reciprocal(recip[:, :, :], sums[:, :, :, HD]))
                settle()
                V.tensor_tensor(v[:, :, :].rearrange("p t (h d) -> p t h d", d=HD), sums[:, :, :, 0:HD],
                                recip[:, :, :].unsqueeze(3).broadcast_to([P, NT, HEADS, HD]), ALU.mult)\
                    .then_inc(y_ready, 1)
                dve.wait_ge(out_mm, i * 2 + 2)
                V.tensor_tensor(h[:, :, :], tiles(0), h[:, :, :], ALU.add).then_inc(x2_ready, 1)
                dve.wait_ge(x2_ready, i + 1)
                layer_norm(LN_X2, h, EPS)

                dve.wait_ge(logits_mm, i + 1)
                step(V.tensor_tensor(logits[:, :, :], bank[:, 1, 0:NT * E].rearrange("p (t e) -> p t e", e=E),
                                     router_b[:, :].unsqueeze(1).broadcast_to([P, NT, E]), ALU.add))
                settle()
                step(V.tensor_reduce(best[:, :], logits[:, :, :], AX, ALU.max))
                settle()
                best_bc = best[:, :].unsqueeze(2).broadcast_to([P, NT, E])
                rank_bc = const("rank").unsqueeze(1).broadcast_to([P, NT, E])
                step(V.tensor_tensor(onehot[:, :, :], logits[:, :, :], best_bc, ALU.is_equal))
                settle()
                step(V.tensor_tensor(onehot[:, :, :], onehot[:, :, :], rank_bc, ALU.mult))
                settle()
                step(V.tensor_reduce(best[:, :], onehot[:, :, :], AX, ALU.min))
                settle()
                step(V.tensor_tensor(onehot[:, :, :], rank_bc, best_bc, ALU.is_equal))
                settle()
                for e in range(E):
                    dve.wait_ge(down_mm, i * E + e + 1)
                    for t in range(NT):
                        last = V.scalar_tensor_tensor(acc[:, t, :], tiles(6 + e % 2)[:, t, :], onehot[:, t, e:e + 1],
                                                      (h if e == 0 else acc)[:, t, :], ALU.mult, ALU.add)
                    last.then_inc(picked, 1)
                    dve.wait_ge(picked, i * E + e + 1)
                dve.wait_ge(stored, 16 * i)
                scaled(1, y_out, acc[:, :, :], 5, x1).then_inc(y_final, 1)
                assert steps[0] == STEPS, steps


def kernel(**inputs):
    import concourse.bacc as bacc
    from concourse.bass_utils import run_bass_kernel_spmd

    g = {k: np.ascontiguousarray(v) for k, v in inputs.items()}
    x = g["L0_attn_x"]
    arrays = {"x": x, "table": constants(x.shape[1]), "cT": np.ascontiguousarray(g["L0_c"].T), "wmod": g["L0_wmod"],
              "ln_cols": np.ascontiguousarray(np.stack([g[k] for k in (
                  "L0_attn_ln_w", "L0_attn_ln_b", "L0_ffn_ln1_w", "L0_ffn_ln1_b", "L0_ffn_ln2_w",
                  "L0_ffn_ln2_b")], axis=1))}
    for k in ("Wq", "Wk", "Wv", "Wo", "Wg1", "Wg2"):
        arrays[k] = g["L0_attn_" + k]
    for k in ("w_qkv", "w_proj", "gate_w", "gate_b", "w1", "w2"):
        arrays[k] = g["L0_ffn_" + k]
    nc = bacc.Bacc("TRN2", target_bir_lowering=False, num_devices=1)
    aps = {k: nc.dram_tensor("in_" + k, v.shape, F32, kind="ExternalInput").ap() for k, v in arrays.items()}
    out = nc.dram_tensor("out_0", x.shape, F32, kind="ExternalOutput").ap()
    scratch = nc.dram_tensor("modulation", (x.shape[0], 6 * P), F32).ap()
    build(nc, aps, out, scratch)
    r = run_bass_kernel_spmd(nc, [{"in_" + k: v for k, v in arrays.items()}], core_ids=[0])
    return r.results[0]["out_0"]
```

```python
from contextlib import ExitStack

import numpy as np

import concourse.bass as bass
from concourse import mybir

F32 = mybir.dt.float32
F32R = mybir.dt.float32r
U32 = mybir.dt.uint32
ALU = mybir.AluOpType
ACT = mybir.ActivationFunctionType
AX = mybir.AxisListType.X

P = 128
HEADS = 16
HD = P // HEADS
E = 8
LN_X, LN_ATTN, LN_X1, LN_H = range(4)
LNS = 4
LINEAR_STEPS, CORE_STEPS, FINISH_STEPS = 44, 8, 17

LAG_S2 = 16 + 8
LAG_PV = 12
SHIFT = 18
LN_X_AT, T_X_AT, QKV_AT, G1_AT, GATE_AT, ROPE_AT, T_QK_AT = 3, 8, (10, 11, 13, 14), 12, 16, 17, 21
CHUNK_AT, CHUNK_SLOTS, UNIT_AT, ATTEND_AT = 30, 10, (0, 1, 2, 4, 6), 8
LN_ATTN_AT, T_ATTN_AT, OUT_AT, LN_X1_AT, LN_H_AT, T_H_AT = 71, 75, 77, 80, 88, 93
END = 1000
UNITS = 19


def go_on(steps, at, slot):
    while at <= slot:
        at = next(steps, END)
    return at
EPS = 1e-5
HG = 4
HJ = HEADS // HG
QR = 32

TILES = 32
SLOT_TILES = TILES + E
RING = 4

TABLE = {}
_at = 0
for _name, _n in (("ident", P), ("causal", P), ("blockdiag", P), ("head_mask", HEADS), ("cos", 4 * HD),
                  ("sin", 4 * HD), ("k_sel", 3), ("q_sel", 3), ("quad_mask", HJ), ("rank", E), ("ones", P),
                  ("tile_starts", TILES), ("slot_tiles", SLOT_TILES), ("before", E * E), ("upto", E * E)):
    TABLE[_name] = (_at, _n)
    _at += _n
TABLE_COLS = _at


def constants(tokens):
    t = np.zeros((P, TABLE_COLS), np.float32)

    def put(name, values):
        a, n = TABLE[name]
        t[:, a:a + n] = np.asarray(values, np.float32).reshape(P, n)

    p = np.arange(P)
    put("ident", np.eye(P))
    put("causal", p[:, None] <= p[None, :])
    put("blockdiag", p[:, None] // HD == p[None, :] // HD)
    put("head_mask", p[:, None] // HD == np.arange(HEADS)[None, :])
    freq = (1.0 / np.float32(10000.0) ** (np.arange(0, HD, 2, dtype=np.float32) / np.float32(HD))).astype(np.float32)
    pos = (np.arange(tokens // P)[None, :, None] * P + p[:, None, None]).astype(np.float32)
    ang = (pos * freq[None, None, :]).astype(np.float32)
    put("cos", 0.5 * np.concatenate([np.cos(ang), np.cos(ang)], -1))
    put("sin", 0.5 * np.concatenate([-np.sin(ang), np.sin(ang)], -1))
    block = p % QR // HD
    put("k_sel", np.stack([np.choose(block, [1, 1, -1, 0]), np.choose(block, [0, 0, 1, 0]),
                           (block == 3) & (p % HD < 2)], -1))
    put("q_sel", np.stack([np.choose(block, [1, -1, 1, 0]), np.choose(block, [0, 1, 0, 0]), 0 * p], -1))
    put("quad_mask", p[:, None] // QR == np.arange(HJ)[None, :])
    put("rank", np.broadcast_to(np.arange(E) - E, (P, E)))
    put("ones", np.ones((P, P)))
    put("tile_starts", np.broadcast_to(P * np.arange(TILES), (P, TILES)))
    put("slot_tiles", np.broadcast_to(np.arange(SLOT_TILES), (P, SLOT_TILES)))
    e = np.arange(E)
    put("before", np.broadcast_to((e[None, :] < e[:, None]).reshape(-1), (P, E * E)))
    put("upto", np.broadcast_to((e[None, :] <= e[:, None]).reshape(-1), (P, E * E)))
    return t


def build(nc, a, out, scratch, residual, z_rows, z_slots, y_slots):
    B, S, D = a["x"].shape
    NT = S // P
    HID = a["w1"].shape[2]
    HT = HID // P
    NQ = HG * HJ * NT
    SCALE = float(1.0 / np.sqrt(HD))
    assert D == P and S == 512 and HT == 4 and NT == 4 and B * NT == TILES and SLOT_TILES % RING == 0

    with ExitStack() as ctx:
        def sb(name, shape, dt=F32):
            return ctx.enter_context(nc.sbuf_tensor(name, shape, dt))

        def sem(name):
            return ctx.enter_context(nc.semaphore(name))

        table = sb("table", [P, TABLE_COLS])

        def const(name):
            s, n = TABLE[name]
            return table[:, s:s + n]

        ident = const("ident")
        attn_w = sb("attn_w", [P, 3 * P])
        gate1_w = sb("gate1_w", [P, HD])
        gate2_w = sb("gate2_w", [HD, P])
        attn_wo = sb("attn_wo", [P, P])
        msa_w = sb("msa_w", [P, 3 * P])
        rep_w = sb("rep_w", [P, 2, HG, HJ, 4, HD])
        proj_w = sb("proj_w", [P, P])
        router_w = sb("router_w", [P, E])
        router_b = sb("router_b", [P, E])
        ln_cols = sb("ln_cols", [P, 6])
        minus_half = sb("minus_half", [P, NT])
        cT = sb("cT", [P, B])
        cth = sb("cth", [P, B])
        mod_bc = sb("mod_bc", [P, 6, P])
        x = sb("x", [P, NT, P])
        stats = sb("stats", [P, NT, 6])
        moments = sb("moments", [P, 3, NT])
        vareps = sb("vareps", [P, NT])
        rstd = sb("rstd", [P, NT])
        norm = sb("norm", [P, NT, P])
        h = sb("h", [P, NT, P])
        hT = sb("hT", [P, S])
        tanh_qk = sb("tanh_qk", [P, NT, 2 * P])
        silu_qk = sb("silu_qk", [P, NT, 2 * P])
        x1_kept = sb("x1_kept", [P, NT, P])
        h_kept = sb("h_kept", [P, NT, P])
        gb_kept = sb("gb_kept", [P, P])
        y = sb("y", [P, NT, P])
        pT = sb("pT", [P, S])
        rot = sb("rot", [P, NT, 2 * P])
        v = sb("v", [P, NT, P])
        tanh_gate = sb("tanh_gate", [P, NT, P])
        qT = sb("qT", [P, S])
        g1T = qT[0:HD, :]
        kT = sb("kT", [P, S])
        exps = sb("exps", [P, 3, HJ, 2, S])
        wide = exps[:, :, :, :, :].rearrange("p a b c d -> p (a b c d)")
        wmod = wide[:, 0:6 * P]
        w1 = wide[:, 0:E * HID].rearrange("p (e n) -> p e n", e=E)
        w2 = wide[:, E * HID:2 * E * HID].rearrange("p (e t n) -> p e t n", e=E, t=HT)
        residual_in = wide[:, 2 * E * HID:2 * E * HID + TILES * P].rearrange("p (t n) -> p t n", n=P)
        q_blocks = sb("q_blocks", [P, 2, HEADS, P])
        spare = q_blocks[:, :, :, :].rearrange("p c h n -> p (c h n)")
        scores_m = sb("scores_m", [P, 4, 4, P])
        state = sb("state", [P, 3, P])
        mod, modt = (spare[0:B, n * 6 * P:(n + 1) * 6 * P] for n in range(2))
        x1 = sb("x1", [P, NT, P])
        vones = sb("vones", [P, NT, HEADS, QR])
        rounded = sb("rounded", [P, 2, S], F32R)
        kq_parts = sb("kq_parts", [P, 2 * HG, S], F32R)
        q_quads = sb("q_quads", [P, HG, HJ, S], F32R)
        negmax = sb("negmax", [P, HG, HJ, NT])
        negmax_hi = sb("negmax_hi", [P, HG, HJ, NT], F32R)
        shift = sb("shift", [P, HG, NT, HJ, 2])
        shiftT = sb("shiftT", [2 * HJ, 2, S], F32R)
        yT = sb("yT", [P, HG, S])
        recip = sb("recip", [P, NT, HEADS])
        logits = sb("logits", [P, NT, E])
        best = sb("best", [P, NT])
        onehot = sb("onehot", [P, NT, E])
        y_out = sb("y_out", [P, NT, P])
        onehots = sb("onehots", [P, TILES, E])
        z_all = residual_in
        y_rows = (x, norm, h, x1, x1_kept, h_kept, v, y)
        used = [0]

        def take(*shape, dt=F32):
            n = int(np.prod(shape))
            part = spare[:, used[0]:used[0] + n]
            used[0] += n
            assert used[0] <= 2 * HEADS * P
            if dt != F32:
                part = part.bitcast(dt)
            return part if len(shape) == 1 else part.rearrange(
                {2: "p (a b) -> p a b", 3: "p (a b c) -> p a b c"}[len(shape)],
                **dict(zip("abc"[1:len(shape)], shape[1:])))

        totals = take(2, TILES, E)
        over = take(E, TILES)
        tiles_of = take(E)
        square = take(E, E)
        starts = take(E)
        ends = take(E)
        place = take(TILES, E)
        slot_f = take(TILES)
        slot = sb("slot", [P, TILES], U32)
        past = take(SLOT_TILES, E)
        expert_f = take(SLOT_TILES)
        expert = sb("expert", [P, SLOT_TILES], U32)
        zeros = y[:, 0, :]
        z_in = take(RING, P)
        zT = take(2, P)
        gelu = yT[:, 0:2]
        geluT = yT[:, 2:4]
        y_tile = take(RING, P)
        gate_b_rows = vones[:, :, :, :].rearrange("p a b c -> p (a b c)")[:, 0:B * P]\
            .rearrange("p (b n) -> p b n", b=B)

        bank = ctx.enter_context(nc.psum_tensor("bank", [P, 8, S], F32))

        loaded = sem("loaded")
        prepared = sem("prepared")
        silu_c = sem("silu_c")
        mod_mm = sem("mod_mm")
        mod_step = sem("mod_step")
        mod_ready = sem("mod_ready")
        x_landed = sem("x_landed")
        mod_landed = sem("mod_landed")
        var_ready = sem("var_ready")
        rstd_ready = sem("rstd_ready")
        norm_ready = sem("norm_ready")
        pool_step = sem("pool_step")
        h_ready = sem("h_ready")
        transposed = sem("transposed")
        hT_ready = sem("hT_ready")
        qkv_mm = sem("qkv_mm")
        tanh_ready = sem("tanh_ready")
        silu_ready = sem("silu_ready")
        g1_mm = sem("g1_mm")
        g1_ready = sem("g1_ready")
        gate_mm = sem("gate_mm")
        gate_ready = sem("gate_ready")
        rot_ready = sem("rot_ready")
        q_transposed = sem("q_transposed")
        k_transposed = sem("k_transposed")
        qT_ready = sem("qT_ready")
        kT_ready = sem("kT_ready")
        blocks_ready = sem("blocks_ready")
        unit_mm = sem("unit_mm")
        unit_taken = sem("unit_taken")
        state_ready = sem("state_ready")
        attn_mm = sem("attn_mm")
        gated = sem("gated")
        out_mm = sem("out_mm")
        x1_ready = sem("x1_ready")
        carried = sem("carried")
        vproj_mm = sem("vproj_mm")
        vones_ready = sem("vones_ready")
        qkproj_mm = sem("qkproj_mm")
        rounded_ready = sem("rounded_ready")
        parts_ready = sem("parts_ready")
        quads_ready = sem("quads_ready")
        max_mm = sem("max_mm")
        max_taken = sem("max_taken")
        shift_ready = sem("shift_ready")
        shift_mm = sem("shift_mm")
        shiftT_ready = sem("shiftT_ready")
        shift_landed = [sem(f"shift_landed{n}") for n in range(2)]
        s2_mm = sem("s2_mm")
        exp_ready = sem("exp_ready")
        pv_mm = sem("pv_mm")
        yT_ready = sem("yT_ready")
        y_transposed = sem("y_transposed")
        y_ready = sem("y_ready")
        p_transposed = sem("p_transposed")
        pT_ready = sem("pT_ready")
        proj_mm = sem("proj_mm")
        x2_ready = sem("x2_ready")
        var2_ready = sem("var2_ready")
        rstd2_ready = sem("rstd2_ready")
        norm2_ready = sem("norm2_ready")
        logits_mm = sem("logits_mm")
        routed = sem("routed")
        kept = sem("kept")
        z_loaded = sem("z_loaded")
        z_stored = sem("z_stored")
        stored = sem("stored")
        dve_step = sem("dve_step")
        zeroed = sem("zeroed")
        counted = sem("counted")
        route_step = sem("route_step")
        slots_ready = sem("slots_ready")
        experts_ready = sem("experts_ready")
        scattered = sem("scattered")
        w_loaded = sem("w_loaded")
        residual_landed = sem("residual_landed")
        z_landed = [sem(f"z_landed{r}") for r in range(RING)]
        z_mm = sem("z_mm")
        zT_done = sem("zT_done")
        up_mm = sem("up_mm")
        gelu_done = sem("gelu_done")
        gelu_mm = sem("gelu_mm")
        geluT_done = sem("geluT_done")
        down_mm = sem("down_mm")
        y_done = sem("y_done")
        y_stored = [sem(f"y_stored{r}") for r in range(RING)]
        gathered = [sem(f"gathered{b}") for b in range(B)]
        final_step = sem("final_step")
        row_done = sem("row_done")
        out_stored = sem("out_stored")

        N_LOADS = 14
        SLOTS = NQ + LAG_S2 + LAG_PV
        block = ctx.enter_context(nc.Block())

        @block.sync
        def _(sp):
            def load(dst, src):
                sp.dma_start(dst, src).then_inc(loaded, 16)

            load(table[:, :], a["table"])
            load(cT[:, :], a["cT"])
            load(wmod, a["wmod"])
            for n, name in enumerate(("Wq", "Wk", "Wv")):
                load(attn_w[:, n * P:(n + 1) * P], a[name])
            load(gate1_w[:, :], a["Wg1"])
            load(gate2_w[:, :], a["Wg2"])
            load(attn_wo[:, :], a["Wo"])
            load(msa_w[:, :], a["w_qkv"])
            load(proj_w[:, :], a["w_proj"])
            load(router_w[:, :], a["gate_w"])
            load(router_b[:, :], a["gate_b"].unsqueeze(0).broadcast_to([P, E]))
            load(ln_cols[:, :], a["ln_cols"])
            sp.wait_ge(mod_ready, 1)
            sp.dma_start(scratch, mod[:, :]).then_inc(stored, 16)
            sp.wait_ge(stored, 16)

            def load_x(row):
                sp.dma_start(x[:, :, :], a["x"][bass.ds(row, 1)].rearrange("a (t p) d -> p (a t) d", p=P))\
                    .then_inc(x_landed, 16)

            def load_mod(row):
                sp.dma_start(mod_bc[:, :, :], scratch[bass.ds(row, 1)].rearrange("a (m d) -> a m d", d=P)
                             .broadcast_to([P, 6, P])).then_inc(mod_landed, 16)

            def softmax_row(i, more):
                if more:
                    sp.wait_ge(x1_ready, i + 1)
                    load_x(i + 1)
                    sp.wait_ge(carried, 3 * i + 3)
                    load_mod(i + 1)
                for g in range(HG):
                    sp.wait_ge(shiftT_ready, i * HG + g + 1)
                    for j in range(HJ):
                        r = QR * j + 3 * HD
                        sp.dma_start(q_quads[r:r + 2, g, j, :].bitcast(F32),
                                     shiftT[2 * j:2 * j + 2, g % 2, :].bitcast(F32)).then_inc(shift_landed[g % 2], 16)
                sp.wait_ge(norm2_ready, i + 1)
                sp.dma_start(z_rows[bass.ds(i, 1)].rearrange("a (t p) d -> p (a t) d", p=P), norm[:, :, :])\
                    .then_inc(z_stored, 16)
                sp.wait_ge(kept, i + 2)
                sp.dma_start(residual[bass.ds(i, 1)].rearrange("a (t p) d -> p (a t) d", p=P), y_out[:, :, :])\
                    .then_inc(stored, 16)

            load_x(0)
            load_mod(0)
            with sp.Fori(0, B - 1) as i:
                softmax_row(i, True)
            softmax_row(B - 1, False)
            sp.wait_ge(yT_ready, HG * B)
            sp.dma_start(w1, a["w1"].rearrange("e p n -> p e n")).then_inc(w_loaded, 16)
            sp.dma_start(w2, a["w2"].rearrange("e (t p) n -> p e t n", p=P)).then_inc(w_loaded, 16)
            sp.wait_ge(z_stored, 16 * B)
            sp.dma_start(z_all, z_rows.rearrange("b (t p) d -> p (b t) d", p=P)).then_inc(z_loaded, 16)
            sp.dma_start(gate_b_rows, scratch[:, 5 * P:6 * P].unsqueeze(0).broadcast_to([P, B, P]))\
                .then_inc(residual_landed, 16)
            sp.wait_ge(scattered, 16 * TILES)
            sp.wait_ge(stored, 16 * (B + 1))
            sp.dma_start(residual_in, residual.rearrange("b (t p) d -> p (b t) d", p=P)).then_inc(residual_landed, 16)

            def load_z(n, ring):
                sp.dma_start(z_in[:, ring, :], z_slots[bass.ds(n * P, P), :]).then_inc(z_landed[ring], 16)

            def store_y(n, ring):
                sp.wait_ge(y_done, n + 1)
                sp.dma_start(y_slots[bass.ds(n * P, P), :], y_tile[:, ring, :]).then_inc(y_stored[ring], 16)

            for n in range(RING):
                load_z(n, n)
            with sp.Fori(1, SLOT_TILES // RING) as k:
                for r in range(RING):
                    sp.wait_ge(z_mm, (k - 1) * RING + r + 1)
                    load_z(k * RING + r, r)
                    store_y((k - 1) * RING + r, r)
            for n in range(SLOT_TILES - RING, SLOT_TILES):
                store_y(n, n % RING)
            for b in range(B):
                sp.wait_ge(row_done, b + 1)
                sp.dma_start(out[b].rearrange("(t p) d -> p t d", p=P), y_rows[b][:, :, :])\
                    .then_inc(out_stored, 16)
            sp.wait_ge(out_stored, 16 * B)

        @block.gpsimd
        def _(pool):
            nc.gpsimd.memset(minus_half[:, :], -0.5).then_inc(prepared, 1)
            nc.gpsimd.memset(zeros[:, :], 0.0).then_inc(zeroed, 1)
            pool.wait_ge(loaded, 16 * N_LOADS)

            def rsqrt(ready, done, count):
                pool.wait_ge(ready, count)
                nc.gpsimd.tensor_tensor(rstd[:, :], vareps[:, :], minus_half[:, :], ALU.pow).then_inc(done, 1)

            def modulate(row, n, scale, bias):
                pool.wait_ge(norm_ready, row * LNS + (LN_X, LN_X1)[n] + 1)
                nc.gpsimd.tensor_tensor(h[:, :, :], norm[:, :, :],
                                        mod_bc[:, scale, :].unsqueeze(1).broadcast_to([P, NT, P]), ALU.mult)\
                    .then_inc(pool_step, 1)
                pool.wait_ge(pool_step, row * 2 + n + 1)
                nc.gpsimd.tensor_tensor(h[:, :, :], h[:, :, :],
                                        mod_bc[:, bias, :].unsqueeze(1).broadcast_to([P, NT, P]), ALU.add)\
                    .then_inc(h_ready, 1)

            def linear_row(row, first):
                rsqrt(var_ready, rstd_ready, row * LNS + LN_X + 1)
                if not first:
                    pool.wait_ge(carried, 3 * row)
                pool.wait_ge(mod_landed, 16 * row + 16)
                modulate(row, 0, 1, 0)
                pool.wait_ge(qT_ready, row + 1)
                for c in range(NT):
                    if c >= 2:
                        pool.wait_ge(unit_mm, row * UNITS + 5 * (c - 1))
                    nc.gpsimd.tensor_tensor(q_blocks[:, c % 2], qT[:, c * P:(c + 1) * P].unsqueeze(1)
                                            .broadcast_to([P, HEADS, P]),
                                            const("head_mask").unsqueeze(2).broadcast_to([P, HEADS, P]), ALU.mult)\
                        .then_inc(blocks_ready, 1)
                rsqrt(var_ready, rstd_ready, row * LNS + LN_ATTN + 1)
                rsqrt(var_ready, rstd_ready, row * LNS + LN_X1 + 1)
                modulate(row, 1, 4, 3)
                rsqrt(var_ready, rstd_ready, row * LNS + LN_H + 1)

            def between(finished, started):
                for g in range(HG):
                    if started is not None:
                        pool.wait_ge(parts_ready, started * 2 * HG + 2 * g + 2)
                        nc.gpsimd.tensor_tensor(q_quads[:, g], kq_parts[:, 2 * g + 1, :].bitcast(F32).unsqueeze(1)
                                                .broadcast_to([P, HJ, S]),
                                                const("quad_mask").unsqueeze(2).broadcast_to([P, HJ, S]), ALU.mult)\
                            .then_inc(quads_ready, 1)
                    if g == 1 and finished is not None:
                        rsqrt(var2_ready, rstd2_ready, finished + 1)

            linear_row(0, True)
            between(None, 0)
            with pool.Fori(0, B - 1) as i:
                linear_row(i + 1, False)
                between(i, i + 1)
            between(B - 1, None)
            pool.wait_ge(slots_ready, 1)
            pool.wait_ge(z_loaded, 16)
            pool.wait_ge(zeroed, 17)
            for t in range(TILES):
                pool.indirect_dma_start(z_slots, bass.IndirectOffsetOnAxis(ap=slot[:, t:t + 1], axis=0),
                                        z_all[:, t, :], None).then_inc(scattered, 16)
            for r in range(RING):
                pool.wait_ge(y_stored[r], 16 * SLOT_TILES // RING)
            for t in range(TILES):
                pool.indirect_dma_start(y_rows[t // NT][:, t % NT, :], None, y_slots,
                                        bass.IndirectOffsetOnAxis(ap=slot[:, t:t + 1], axis=0))\
                    .then_inc(gathered[t // NT], 16)

        @block.scalar
        def _(act):
            act.wait_ge(zeroed, 1)
            act.dma_start(z_slots.rearrange("(t p) d -> p t d", p=P),
                          zeros[:, :].unsqueeze(1).broadcast_to([P, SLOT_TILES, P])).then_inc(zeroed, 16)
            act.wait_ge(loaded, 16 * N_LOADS)
            nc.scalar.activation(cth[:, :], cT[:, :], ACT.Tanh, scale=0.5).then_inc(silu_c, 1)

            def copy_T(row, n, w, b):
                act.wait_ge(transposed, row * 3 + n + 1)
                nc.scalar.activation(hT[:, :], bank[:, 5, :], ACT.Identity, scale=w, bias=b).then_inc(hT_ready, 1)

            def linear_row(row):
                yield T_X_AT + 1
                copy_T(row, 0, 1.0, 0.0)
                for t in range(NT):
                    yield QKV_AT[t] + 1
                    act.wait_ge(qkv_mm, row * NT + t + 1)
                    nc.scalar.activation(tanh_qk[:, t, :], bank[:, 6 + t % 2, 0:2 * P], ACT.Tanh, scale=0.5)\
                        .then_inc(tanh_ready, 1)
                yield GATE_AT + 2
                act.wait_ge(gate_mm, row + 1)
                nc.scalar.activation(tanh_gate[:, :, :].rearrange("p t n -> p (t n)"), bank[:, 5, :], ACT.Tanh,
                                     scale=0.5).then_inc(gate_ready, 1)
                yield T_QK_AT + 1
                act.wait_ge(q_transposed, row + 1)
                nc.scalar.activation(qT[:, :], bank[:, 6, :], ACT.Identity).then_inc(qT_ready, 1)
                yield T_QK_AT + 2
                act.wait_ge(k_transposed, row + 1)
                nc.scalar.activation(kT[:, :], bank[:, 7, :], ACT.Identity).then_inc(kT_ready, 1)
                yield T_ATTN_AT + 1
                copy_T(row, 1, ln_cols[:, 0:1], ln_cols[:, 1:2])
                yield T_H_AT + 1
                copy_T(row, 2, ln_cols[:, 2:3], ln_cols[:, 3:4])

            def round_part(row, r):
                act.wait_ge(qkproj_mm, row * 2 * HG + r + 1)
                if r >= 2:
                    act.wait_ge(parts_ready, row * 2 * HG + r - 1)
                sel = const(("k_sel", "q_sel")[r % 2])
                nc.scalar.activation(rounded[:, r % 2, :], bank[:, 5 + r % 3, :], ACT.Identity,
                                     scale=sel[:, 0:1], bias=sel[:, 2:3]).then_inc(rounded_ready, 1)

            def copy_p(row, n, w, b):
                act.wait_ge(p_transposed, row * 2 + n + 1)
                nc.scalar.activation(pT[:, :], bank[:, 2 * n, :], ACT.Identity, scale=w, bias=b).then_inc(pT_ready, 1)

            def between(finished, started):
                for r in range(2 * HG):
                    if started is not None:
                        round_part(started, r)
                    if r == 2 and finished is not None:
                        copy_p(finished, 0, 1.0, 0.0)
                if finished is not None:
                    copy_p(finished, 1, ln_cols[:, 4:5], ln_cols[:, 5:6])

            def softmax_row(i, other):
                act.wait_ge(kept, i + 1)
                nc.scalar.activation(h_kept[:, :, :], h[:, :, :], ACT.Identity).then_inc(carried, 1)
                nc.scalar.activation(x1_kept[:, :, :], x1[:, :, :], ACT.Identity).then_inc(carried, 1)
                nc.scalar.activation(gb_kept[:, :], mod_bc[:, 5, :], ACT.Identity).then_inc(carried, 1)
                at = 0
                for s in range(SLOTS):
                    at = go_on(other, at, s)
                    m = s - LAG_S2
                    if 0 <= m < NQ:
                        w, j, n = m // 8, m // 2 % HJ, m % 2
                        act.wait_ge(s2_mm, i * NQ + m + 1)
                        if m % 8 == 0 and w >= 3:
                            act.wait_ge(pv_mm, i * 2 * HG + w - 2)
                        nc.scalar.activation(exps[:, w % 3, j, n, :], bank[:, 2 + m % 2, :], ACT.Exp, scale=SCALE)\
                            .then_inc(exp_ready, 1)
                    if m >= 27 and m % 16 == 11:
                        g = (m - 27) // 16
                        act.wait_ge(pv_mm, i * 2 * HG + 2 * g + 2)
                        nc.scalar.activation(yT[:, g, :], bank[:, 4, :], ACT.Identity).then_inc(yT_ready, 1)
                go_on(other, at, END - 1)

            go_on(linear_row(0), 0, END - 1)
            between(None, 0)
            with act.Fori(0, B - 1) as i:
                softmax_row(i, linear_row(i + 1))
                between(i, i + 1)
            softmax_row(B - 1, iter(()))
            between(B - 1, None)

            def copy_z(n, r):
                act.wait_ge(z_mm, n + 1)
                nc.scalar.activation(zT[:, r % 2, :], bank[:, r % 2, 0:P], ACT.Identity, scale=ln_cols[:, 4:5],
                                     bias=ln_cols[:, 5:6]).then_inc(zT_done, 1)

            def activate(n, r):
                act.wait_ge(up_mm, n + 1)
                nc.scalar.activation(gelu[:, r % 2], bank[:, 2 + r % 2, :], ACT.Gelu_apprx_tanh)\
                    .then_inc(gelu_done, 1)

            copy_z(0, 0)
            for n in range(RING):
                copy_z(n + 1, n + 1)
                activate(n, n)
            with act.Fori(1, SLOT_TILES // RING - 1) as k:
                for r in range(RING):
                    copy_z(k * RING + r + 1, r + 1)
                    activate(k * RING + r, r)
            for n in range(SLOT_TILES - RING, SLOT_TILES):
                if n + 1 < SLOT_TILES:
                    copy_z(n + 1, n + 1)
                activate(n, n)
        @block.tensor
        def _(pe):
            mm = nc.tensor.matmul
            pe.wait_ge(silu_c, 2)
            mm(bank[0:B, 0, :], cth[:, :], wmod[:, 0:S], start=True, stop=True)
            mm(bank[0:B, 1, 0:2 * P], cth[:, :], wmod[:, S:6 * P], start=True, stop=True).then_inc(mod_mm, 1)
            pe.wait_ge(loaded, 16 * N_LOADS)
            pe.wait_ge(prepared, 12)

            def tile(T, t):
                return T[:, t * P:(t + 1) * P]

            def transpose_tiles(b, src, signal):
                for t in range(NT):
                    last = nc.tensor.transpose(tile(bank[:, b, :], t), src(t), ident)
                last.then_inc(signal, 1)

            def unit(row, c, n):
                u = 5 * c + (n if c < NT - 1 or n == 0 else n - 1)
                if u >= 2:
                    pe.wait_ge(unit_taken, row * UNITS + u - 1)
                if n == 1:
                    last = mm(bank[:, 6 + u % 2, 0:P], rot[:, c, P:2 * P], v[:, c, :], start=True, stop=True)
                else:
                    if n == 0:
                        pe.wait_ge(blocks_ready, row * NT + c + 1)
                    q = max(n - 1, 0)
                    last = mm(bank[:, 6 + u % 2, :], tile(kT, c), q_blocks[:, c % 2, 4 * q:4 * q + 4, :]
                              .rearrange("p h n -> p (h n)"), start=True, stop=True)
                last.then_inc(unit_mm, 1)

            def attend(row, c, core):
                if c >= 1:
                    pe.wait_ge(gated, row * NT + c)
                if core is not None and c != 1:
                    pe.wait_ge(shiftT_ready, core * HG + (2, 0, 3, 4)[c])
                if c >= 2:
                    pe.wait_ge(state_ready, row * (NT - 2) + c - 1)
                pe.wait_ge(unit_taken, row * UNITS + min(5 * (c + 1), UNITS))
                if c >= 1:
                    mm(bank[:, 5, 0:P], tile(qT, c), state[:, c - 1, :], start=True, stop=False,
                       skip_group_check=True)
                for hh in range(HEADS):
                    at = slice(hh * HD, (hh + 1) * HD)
                    last = mm(bank[:, 5, at], scores_m[:, hh // 4, hh % 4, :], v[:, c, at],
                              start=c == 0, stop=True, skip_group_check=True)
                last.then_inc(attn_mm, 1)

            def linear_row(row, core):
                yield T_X_AT
                pe.wait_ge(h_ready, row * 2 + 1)
                transpose_tiles(5, lambda t: h[:, t, :], transposed)
                for t in range(NT):
                    yield QKV_AT[t]
                    if t == 0:
                        pe.wait_ge(hT_ready, row * 3 + 1)
                    if t >= 2:
                        pe.wait_ge(silu_ready, row * NT + t - 1)
                    mm(bank[:, 6 + t % 2, 0:3 * P], tile(hT, t), attn_w[:, :], start=True, stop=True)\
                        .then_inc(qkv_mm, 1)
                    if t == 1:
                        yield G1_AT
                        mm(bank[0:HD, 5, :], gate1_w[:, :], hT[:, :], start=True, stop=True).then_inc(g1_mm, 1)
                yield GATE_AT
                pe.wait_ge(g1_ready, row + 1)
                for t in range(NT):
                    last = mm(tile(bank[:, 5, :], t), tile(g1T, t), gate2_w[:, :], start=True, stop=True)
                last.then_inc(gate_mm, 1)
                yield T_QK_AT
                pe.wait_ge(rot_ready, row + 1)
                transpose_tiles(6, lambda t: rot[:, t, 0:P], q_transposed)
                yield T_QK_AT + 1
                transpose_tiles(7, lambda t: rot[:, t, P:2 * P], k_transposed)
                for c in range(NT):
                    for n in range(5):
                        if n != 1 or c < NT - 1:
                            yield CHUNK_AT + CHUNK_SLOTS * c + UNIT_AT[n]
                            if c == n == 0:
                                pe.wait_ge(kT_ready, row + 1)
                            unit(row, c, n)
                    yield CHUNK_AT + CHUNK_SLOTS * c + ATTEND_AT
                    attend(row, c, core)
                yield T_ATTN_AT
                pe.wait_ge(norm_ready, row * LNS + LN_ATTN + 1)
                transpose_tiles(5, lambda t: norm[:, t, :], transposed)
                yield OUT_AT
                pe.wait_ge(hT_ready, row * 3 + 2)
                for t in range(NT):
                    last = mm(tile(bank[:, 6, :], t), tile(hT, t), attn_wo[:, :], start=True, stop=True)
                last.then_inc(out_mm, 1)
                yield T_H_AT
                pe.wait_ge(norm_ready, row * LNS + LN_H + 1)
                transpose_tiles(5, lambda t: norm[:, t, :], transposed)

            def project(row, r):
                if r >= 3:
                    pe.wait_ge(parts_ready, row * 2 * HG + r - 2)
                mm(bank[:, 5 + r % 3, :], rep_w[:, 1 - r % 2, r // 2].rearrange("p j c d -> p (j c d)"),
                   hT[:, :], start=True, stop=True).then_inc(qkproj_mm, 1)

            def between(finished, started):
                if finished is not None:
                    pe.wait_ge(yT_ready, finished * HG + HG)
                    for t in range(NT):
                        for g in range(HG):
                            last = nc.tensor.transpose(tile(bank[:, t, :], g), tile(yT[:, g], t), ident)
                    last.then_inc(y_transposed, 1)
                if started is not None:
                    pe.wait_ge(hT_ready, started * 3 + 3)
                    for t in range(NT):
                        last = mm(tile(bank[:, 4, :], t), tile(hT, t), msa_w[:, 2 * P:3 * P], start=True, stop=True)
                    last.then_inc(vproj_mm, 1)
                    for r in range(3):
                        project(started, r)
                if finished is not None:
                    pe.wait_ge(y_ready, finished + 1)
                    transpose_tiles(0, lambda t: y[:, t, :], p_transposed)
                if started is not None:
                    project(started, 3)
                    project(started, 4)
                if finished is not None:
                    pe.wait_ge(pT_ready, finished * 2 + 1)
                    for t in range(NT):
                        last = mm(tile(bank[:, 1, :], t), tile(pT, t), proj_w[:, :], start=True, stop=True)
                    last.then_inc(proj_mm, 1)
                if started is not None:
                    for r in range(5, 2 * HG):
                        project(started, r)
                if finished is not None:
                    pe.wait_ge(norm2_ready, finished + 1)
                    transpose_tiles(2, lambda t: norm[:, t, :], p_transposed)
                    pe.wait_ge(pT_ready, finished * 2 + 2)
                    for t in range(NT):
                        last = mm(bank[:, 3, t * E:(t + 1) * E], tile(pT, t), router_w[:, :], start=True, stop=True)
                    last.then_inc(logits_mm, 1)

            def k_part(g):
                return kq_parts[:, 2 * g, :]

            def max_scores(i, a):
                g, j, t = a // (HJ * NT), a // NT % HJ, a % NT
                if j == t == 0:
                    pe.wait_ge(quads_ready, i * HG + g + 1)
                if a >= 2:
                    pe.wait_ge(max_taken, i * NQ + a - 1)
                mm(bank[:, a % 2, :], tile(q_quads[:, g, j], t), k_part(g), start=True, stop=True)\
                    .then_inc(max_mm, 1)

            def shift_rows(i, g, more):
                pe.wait_ge(shift_ready, i * HG + g + 1)
                if g >= 1:
                    pe.wait_ge(shiftT_ready, i * HG + g)
                if more and g == 0:
                    pe.wait_ge(gate_ready, i + 2)
                if more and g >= 2:
                    pe.wait_ge(gated, (i + 1) * NT + g)
                for t in range(NT):
                    last = mm(tile(bank[0:2 * HJ, 5, :], t), shift[:, g, t].rearrange("p j s -> p (j s)"),
                              ident, start=True, stop=True)
                last.then_inc(shift_mm, 1)

            def shifted_scores(i, m):
                w, j, n = m // 8, m // 2 % HJ, m % 2
                g, half = divmod(w, 2)
                if m % 16 == 0:
                    pe.wait_ge(shift_landed[g % 2], i * 16 * HJ * 2 + 16 * HJ * (g // 2 + 1))
                if m >= 2:
                    pe.wait_ge(exp_ready, i * NQ + m - 1)
                mm(bank[:, 2 + m % 2, :], tile(k_part(g), 2 * half + n), q_quads[:, g, j],
                   start=True, stop=True).then_inc(s2_mm, 1)

            def weighted_values(i, n):
                w, k, j = n // 8, n // 4 % 2, n % 4
                g, half = divmod(w, 2)
                if n % 8 == 0:
                    pe.wait_ge(exp_ready, i * NQ + 8 * (w + 1))
                    if g >= 1 and half == 0:
                        pe.wait_ge(yT_ready, i * HG + g)
                    if n == 0:
                        pe.wait_ge(vones_ready, i + 1)
                last = mm(bank[QR * j:QR * (j + 1), 4, :], vones[:, 2 * half + k, HJ * g + j, :],
                          exps[:, w % 3, j, k, :], start=half == 0 and k == 0, stop=half == 1 and k == 1)
                if n % 8 == 7:
                    last.then_inc(pv_mm, 1)

            def softmax_row(i, other, more):
                at = 0
                for s in range(SLOTS):
                    at = go_on(other, at, s)
                    if s < NQ:
                        max_scores(i, s)
                    if s % 16 == SHIFT % 16 and SHIFT <= s < SHIFT + 16 * HG:
                        shift_rows(i, (s - SHIFT) // 16, more)
                    if 0 <= s - LAG_S2 < NQ:
                        shifted_scores(i, s - LAG_S2)
                    if 0 <= s - LAG_S2 - LAG_PV:
                        weighted_values(i, s - LAG_S2 - LAG_PV)
                go_on(other, at, END - 1)

            go_on(linear_row(0, None), 0, END - 1)
            between(None, 0)
            with pe.Fori(0, B - 1) as i:
                softmax_row(i, linear_row(i + 1, i), True)
                between(i, i + 1)
            softmax_row(B - 1, iter(()), False)
            between(B - 1, None)

            pe.wait_ge(routed, B)
            flat = onehots[:, :, :].rearrange("p t e -> p (t e)")
            mm(bank[:, 0, 0:TILES * E], const("causal"), flat, start=True, stop=True)
            mm(bank[:, 1, 0:TILES * E], const("ones"), flat, start=True, stop=True).then_inc(counted, 1)

            def transpose_z(k, r):
                k, r = k + r // RING, r % RING
                pe.wait_ge(z_landed[r], 16 * (k + 1))
                nc.tensor.transpose(bank[:, r % 2, 0:P], z_in[:, r, :], ident).then_inc(z_mm, 1)

            def expert_of(n):
                return pe.value_load(expert[0:1, bass.ds(n, 1)], min_val=0, max_val=E - 1)

            def up(n, r, first):
                e = expert_of(n)
                pe.wait_ge(zT_done, n + 1)
                if not first:
                    pe.wait_ge(gelu_done, n - 1)
                mm(bank[:, 2 + r % 2, :], zT[:, r % 2, :], w1[:, bass.ds(e, 1), :]
                   .rearrange("p a n -> p (a n)"), start=True, stop=True).then_inc(up_mm, 1)

            def transpose_gelu(n, r):
                pe.wait_ge(gelu_done, n + 1)
                for t in range(HT):
                    last = nc.tensor.transpose(bank[:, 4 + r % 2, t * P:(t + 1) * P],
                                               gelu[:, r % 2, t * P:(t + 1) * P], ident)
                last.then_inc(gelu_mm, 1)

            def down(n, r, first):
                e = expert_of(n)
                pe.wait_ge(geluT_done, n + 1)
                if not first:
                    pe.wait_ge(y_done, n - 1)
                for t in range(HT):
                    last = mm(bank[:, 6 + r % 2, 0:P], geluT[:, r % 2, t * P:(t + 1) * P],
                              w2[:, bass.ds(e, 1), t, :].rearrange("p a n -> p (a n)"),
                              start=t == 0, stop=t == HT - 1)
                last.then_inc(down_mm, 1)

            pe.wait_ge(experts_ready, 1)
            pe.wait_ge(w_loaded, 32)
            transpose_z(0, 0)
            for n in range(RING):
                transpose_z(0, n + 1)
                up(n, n, n < 2)
                if n >= 1:
                    transpose_gelu(n - 1, n - 1)
                if n >= 2:
                    down(n - 2, n - 2, n < 4)
            with pe.Fori(1, SLOT_TILES // RING - 1) as k:
                for r in range(RING):
                    transpose_z(k, r + 1)
                    up(k * RING + r, r, False)
                    transpose_gelu(k * RING + r - 1, r - 1)
                    down(k * RING + r - 2, r - 2, False)
            for n in range(SLOT_TILES - RING, SLOT_TILES + 2):
                if n + 1 < SLOT_TILES:
                    transpose_z(0, n + 1)
                if n < SLOT_TILES:
                    up(n, n, False)
                if n - 1 < SLOT_TILES:
                    transpose_gelu(n - 1, n - 1)
                down(n - 2, n - 2, False)

        @block.vector
        def _(dve):
            V = nc.vector
            dve.wait_ge(silu_c, 1)
            V.scalar_tensor_tensor(cth[:, :], cth[:, :], 1.0, cT[:, :], ALU.add, ALU.mult).then_inc(silu_c, 1)
            V.memset(rep_w[:, :, :, :, :, :].rearrange("p a b c d e -> p (a b c d e)"), 0.0).then_inc(prepared, 1)
            V.memset(vones[:, :, :, :].rearrange("p a b c -> p (a b c)"), 0.0).then_inc(prepared, 1)
            dve.wait_ge(prepared, 3)
            V.memset(vones[:, :, :, HD:HD + 1].rearrange("p a b c -> p (a b c)"), 1.0).then_inc(prepared, 1)
            for part in range(2):
                for g in range(HG):
                    src = msa_w[:, part * P + g * QR:part * P + (g + 1) * QR].rearrange("p (j d) -> p j d", d=HD)
                    V.tensor_copy(rep_w[:, part, g, :, 0:3, :], src.unsqueeze(2).broadcast_to([P, HJ, 3, HD]))\
                        .then_inc(prepared, 1)
            dve.wait_ge(mod_mm, 1)
            V.tensor_scalar(mod[:, 0:S], bank[0:B, 0, :], 0.5, None, ALU.mult).then_inc(mod_step, 1)
            V.tensor_scalar(mod[:, S:6 * P], bank[0:B, 1, 0:2 * P], 0.5, None, ALU.mult).then_inc(mod_step, 1)
            dve.wait_ge(mod_step, 2)
            for n, m in enumerate((1, 4)):
                V.tensor_scalar(mod[:, m * P:(m + 1) * P], mod[:, m * P:(m + 1) * P], 1.0, None, ALU.add)\
                    .then_inc(mod_step, 1)
            for n, m in enumerate((2, 5)):
                V.tensor_scalar(modt[:, m * P:(m + 1) * P], mod[:, m * P:(m + 1) * P], 0.0, 2.0, ALU.is_ge,
                                ALU.mult).then_inc(mod_step, 1)
            for n, m in enumerate((2, 5)):
                gate = mod[:, m * P:(m + 1) * P]
                dve.wait_ge(mod_step, 6 + 3 * n)
                V.scalar_tensor_tensor(gate, gate, -1.0, gate, ALU.mult, ALU.max).then_inc(mod_step, 1)
                dve.wait_ge(mod_step, 7 + 3 * n)
                V.tensor_scalar(gate, gate, 0.25, None, ALU.max).then_inc(mod_step, 1)
                dve.wait_ge(mod_step, 8 + 3 * n)
                V.scalar_tensor_tensor(gate, modt[:, m * P:(m + 1) * P], -1.0, gate, ALU.add, ALU.mult)\
                    .then_inc(mod_step, 1)
            dve.wait_ge(mod_step, 12)
            V.memset(y_out[:, 0, 1:2], 0.0).then_inc(kept, 1)
            V.memset(y_out[:, 0, 2:3], 0.0).then_inc(mod_ready, 1)
            dve.wait_ge(prepared, 12)
            steps = [0, 0]

            def step(instruction):
                steps[1] += 1
                instruction.then_inc(dve_step, 1)

            def settle():
                dve.wait_ge(dve_step, steps[0] + steps[1])

            def variances(src, eps, signal):
                for t in range(NT):
                    step(V.bn_stats(stats[:, t, :], src[:, t, :]))
                settle()
                (mean_e, var_e), (mean_o, var_o) = ((stats[:, :, n], stats[:, :, n + 1]) for n in (1, 4))
                mean, diff, var = (moments[:, n, :] for n in range(3))
                step(V.tensor_tensor(mean, mean_e, mean_o, ALU.add))
                step(V.tensor_tensor(diff, mean_e, mean_o, ALU.subtract))
                step(V.tensor_tensor(var, var_e, var_o, ALU.add))
                settle()
                step(V.tensor_scalar(mean, mean, 0.5, None, ALU.mult))
                step(V.tensor_tensor(diff, diff, diff, ALU.mult))
                step(V.tensor_scalar(var, var, 1.0 / P, eps, ALU.mult, ALU.add))
                settle()
                V.scalar_tensor_tensor(vareps[:, :], diff, 0.25, var, ALU.mult, ALU.add).then_inc(signal, 1)

            def normalize(src, rstd_signal, count, signal):
                dve.wait_ge(rstd_signal, count)
                for t in range(NT):
                    last = V.tensor_scalar(norm[:, t, :], src[:, t, :], moments[:, 0, t:t + 1], rstd[:, t:t + 1],
                                           ALU.subtract, ALU.mult)
                last.then_inc(signal, 1)

            def layer_norm(row, n, src, eps):
                variances(src, eps, var_ready)
                yield (LN_X_AT, LN_ATTN_AT, LN_X1_AT, LN_H_AT)[n] + 2
                normalize(src, rstd_ready, row * LNS + n + 1, norm_ready)

            def scaled(dst, src, scale, plus):
                step(V.tensor_tensor(dst[:, :, :], src, scale.unsqueeze(1).broadcast_to([P, NT, P]), ALU.mult))
                settle()
                return V.tensor_tensor(dst[:, :, :], dst[:, :, :], plus[:, :, :], ALU.add)

            def tiles(b):
                return bank[:, b, :].rearrange("p (t n) -> p t n", n=P)

            def take_unit(row, c, n):
                u = 5 * c + (n if c < NT - 1 or n == 0 else n - 1)
                dve.wait_ge(unit_mm, row * UNITS + u + 1)
                if n == 1:
                    V.tensor_tensor(state[:, c, :], bank[:, 6 + u % 2, 0:P], const("blockdiag"), ALU.mult)\
                        .then_inc(unit_taken, 1)
                    if c >= 1:
                        dve.wait_ge(unit_taken, row * UNITS + u + 1)
                        V.tensor_tensor(state[:, c, :], state[:, c, :], state[:, c - 1, :], ALU.add)\
                            .then_inc(state_ready, 1)
                    return
                if n == 0 and c >= 1:
                    dve.wait_ge(attn_mm, row * NT + c)
                V.tensor_tensor(scores_m[:, max(n - 1, 0)],
                                bank[:, 6 + u % 2, :].rearrange("p (h n) -> p h n", n=P),
                                const("causal").unsqueeze(1).broadcast_to([P, 4, P]), ALU.mult)\
                    .then_inc(unit_taken, 1)

            def linear_row(row, first):
                yield LN_X_AT
                dve.wait_ge(x_landed, 16 * row + 16)
                yield from layer_norm(row, LN_X, x, EPS)
                for t in range(NT):
                    yield QKV_AT[t] + 2
                    dve.wait_ge(tanh_ready, row * NT + t + 1)
                    V.tensor_copy(v[:, t, :], bank[:, 6 + t % 2, 2 * P:3 * P])
                    V.scalar_tensor_tensor(silu_qk[:, t, :], tanh_qk[:, t, :], 1.0, bank[:, 6 + t % 2, 0:2 * P],
                                           ALU.add, ALU.mult).then_inc(silu_ready, 1)
                    if t == 1:
                        yield G1_AT + 2
                        dve.wait_ge(g1_mm, row + 1)
                        V.tensor_copy(g1T[:, :], bank[0:HD, 5, :]).then_inc(g1_ready, 1)
                heads = silu_qk[:, :, :].rearrange("p t (h d) -> p t h d", d=HD)
                cross = tanh_qk[:, :, :].rearrange("p t (h d) -> p t h d", d=HD)
                hd2 = HD // 2
                cos = const("cos").rearrange("p (t d) -> p t d", d=HD).unsqueeze(2)
                sin = const("sin").rearrange("p (t d) -> p t d", d=HD).unsqueeze(2)
                yield ROPE_AT
                dve.wait_ge(silu_ready, row * NT + NT)
                step(V.tensor_tensor(rot[:, :, :].rearrange("p t (h d) -> p t h d", d=HD), heads,
                                     cos.broadcast_to([P, NT, 2 * HEADS, HD]), ALU.mult))
                for d0, d1 in ((0, hd2), (hd2, 0)):
                    yield ROPE_AT + 1 + d0 // hd2
                    step(V.tensor_tensor(cross[:, :, :, d0:d0 + hd2], heads[:, :, :, d1:d1 + hd2],
                                         sin[:, :, :, d0:d0 + hd2].broadcast_to([P, NT, 2 * HEADS, hd2]), ALU.mult))
                yield ROPE_AT + 3
                settle()
                V.tensor_tensor(rot[:, :, :], rot[:, :, :], tanh_qk[:, :, :], ALU.add).then_inc(rot_ready, 1)
                for c in range(NT):
                    for n in range(5):
                        if n != 1 or c < NT - 1:
                            yield CHUNK_AT + CHUNK_SLOTS * c + UNIT_AT[n] + 1
                            take_unit(row, c, n)
                    yield CHUNK_AT + CHUNK_SLOTS * c + ATTEND_AT + 1
                    if c == 0:
                        dve.wait_ge(gate_ready, row + 1)
                    dve.wait_ge(attn_mm, row * NT + c + 1)
                    V.scalar_tensor_tensor(h[:, c, :], tanh_gate[:, c, :], 1.0, bank[:, 5, 0:P],
                                           ALU.add, ALU.mult).then_inc(gated, 1)
                yield LN_ATTN_AT
                dve.wait_ge(gated, row * NT + NT)
                yield from layer_norm(row, LN_ATTN, h, 4 * EPS)
                yield LN_X1_AT
                dve.wait_ge(out_mm, row + 1)
                if not first:
                    dve.wait_ge(carried, 3 * row)
                scaled(x1, tiles(6), mod_bc[:, 2, :], x).then_inc(x1_ready, 1)
                dve.wait_ge(x1_ready, row + 1)
                yield from layer_norm(row, LN_X1, x1, EPS)
                yield LN_H_AT
                dve.wait_ge(h_ready, row * 2 + 2)
                yield from layer_norm(row, LN_H, h, EPS)

            def part(row, r):
                dve.wait_ge(rounded_ready, row * 2 * HG + r + 1)
                V.scalar_tensor_tensor(kq_parts[:, r, :], bank[:, 5 + r % 3, :],
                                       const(("k_sel", "q_sel")[r % 2])[:, 1:2],
                                       rounded[:, r % 2, :].bitcast(F32), ALU.mult, ALU.add)\
                    .then_inc(parts_ready, 1)

            def between(finished, started):
                if finished is not None:
                    dve.wait_ge(y_transposed, finished + 1)
                    sums = bank[:, 0:4, :].rearrange("p t (h r) -> p t h r", r=QR)
                    step(V.reciprocal(recip[:, :, :], sums[:, :, :, HD]))
                    settle()
                    V.tensor_tensor(y[:, :, :].rearrange("p t (h d) -> p t h d", d=HD), sums[:, :, :, 0:HD],
                                    recip[:, :, :].unsqueeze(3).broadcast_to([P, NT, HEADS, HD]), ALU.mult)\
                        .then_inc(y_ready, 1)
                if started is not None:
                    dve.wait_ge(vproj_mm, started + 1)
                    V.tensor_copy(vones[:, :, :, 0:HD],
                                  bank[:, 4, :].rearrange("p (t h d) -> p t h d", h=HEADS, d=HD))\
                        .then_inc(vones_ready, 1)
                    for r in range(3):
                        part(started, r)
                if finished is not None:
                    dve.wait_ge(proj_mm, finished + 1)
                    V.tensor_tensor(h_kept[:, :, :], tiles(1), h_kept[:, :, :], ALU.add).then_inc(x2_ready, 1)
                if started is not None:
                    part(started, 3)
                    part(started, 4)
                if finished is not None:
                    dve.wait_ge(x2_ready, finished + 1)
                    variances(h_kept, EPS, var2_ready)
                if started is not None:
                    for r in range(5, 2 * HG):
                        part(started, r)
                if finished is None:
                    return
                rows = bass.ds(finished * NT, NT)
                normalize(h_kept, rstd2_ready, finished + 1, norm2_ready)
                dve.wait_ge(stored, 16 * finished + 16)
                scaled(y_out, h_kept[:, :, :], gb_kept[:, :], x1_kept).then_inc(kept, 1)
                dve.wait_ge(logits_mm, finished + 1)
                step(V.tensor_tensor(logits[:, :, :], bank[:, 3, 0:NT * E].rearrange("p (t e) -> p t e", e=E),
                                     router_b[:, :].unsqueeze(1).broadcast_to([P, NT, E]), ALU.add))
                settle()
                step(V.tensor_reduce(best[:, :], logits[:, :, :], AX, ALU.max))
                settle()
                best_bc = best[:, :].unsqueeze(2).broadcast_to([P, NT, E])
                rank_bc = const("rank").unsqueeze(1).broadcast_to([P, NT, E])
                step(V.tensor_tensor(onehot[:, :, :], logits[:, :, :], best_bc, ALU.is_equal))
                settle()
                step(V.tensor_tensor(onehot[:, :, :], onehot[:, :, :], rank_bc, ALU.mult))
                settle()
                step(V.tensor_reduce(best[:, :], onehot[:, :, :], AX, ALU.min))
                settle()
                dve.wait_ge(z_stored, 16 * finished + 16)
                V.tensor_tensor(onehots[:, rows, :], rank_bc, best_bc, ALU.is_equal).then_inc(routed, 1)

            def split_maxima(i, g):
                dve.wait_ge(max_taken, i * NQ + 16 * (g + 1))
                step(V.tensor_copy(negmax_hi[:, g], negmax[:, g]))
                settle()
                hi = negmax_hi[:, g].bitcast(F32).rearrange("p j t -> p t j")
                step(V.tensor_copy(shift[:, g, :, :, 0], hi))
                V.tensor_tensor(shift[:, g, :, :, 1], negmax[:, g].rearrange("p j t -> p t j"), hi,
                                ALU.subtract).then_inc(shift_ready, 1)

            def softmax_row(i, other):
                at = 0
                for s in range(SLOTS):
                    at = go_on(other, at, s)
                    if s < NQ:
                        g, j, t = s // (HJ * NT), s // NT % HJ, s % NT
                        dve.wait_ge(max_mm, i * NQ + s + 1)
                        V.tensor_reduce(negmax[:, g, j, t:t + 1], bank[:, s % 2, :], AX, ALU.max, negate=True)\
                            .then_inc(max_taken, 1)
                        if s % 16 == 15:
                            split_maxima(i, g)
                    if s % 16 == SHIFT % 16 and SHIFT <= s < SHIFT + 16 * HG:
                        g = (s - SHIFT) // 16
                        dve.wait_ge(shift_mm, i * HG + g + 1)
                        if g >= 2:
                            dve.wait_ge(shift_landed[g % 2], i * 16 * HJ * 2 + 16 * HJ)
                        V.tensor_copy(shiftT[:, g % 2, :], bank[0:2 * HJ, 5, :]).then_inc(shiftT_ready, 1)
                go_on(other, at, END - 1)

            go_on(linear_row(0, True), 0, END - 1)
            between(None, 0)
            dve.wait_ge(zeroed, 17)
            assert steps[1] == LINEAR_STEPS, steps
            with dve.Fori(0, B - 1) as i:
                steps[:] = [i * (LINEAR_STEPS + CORE_STEPS + FINISH_STEPS) + LINEAR_STEPS, 0]
                softmax_row(i, linear_row(i + 1, False))
                between(i, i + 1)
                assert steps[1] == LINEAR_STEPS + CORE_STEPS + FINISH_STEPS, steps
            steps[:] = [(B - 1) * (LINEAR_STEPS + CORE_STEPS + FINISH_STEPS) + LINEAR_STEPS, 0]
            softmax_row(B - 1, iter(()))
            between(B - 1, None)
            settle()

            count = [0]

            def route(instruction):
                count[0] += 1
                instruction.then_inc(route_step, 1)
                dve.wait_ge(route_step, count[0])

            def by_tile(b):
                return bank[:, b, 0:TILES * E].rearrange("p (t e) -> p t e", e=E)

            dve.wait_ge(counted, 1)
            route(V.tensor_copy(totals[:, 0], by_tile(1)))
            src, ahead = 0, 1
            while ahead < TILES:
                V.tensor_copy(totals[:, 1 - src, 0:ahead], totals[:, src, 0:ahead])\
                    .then_inc(route_step, 1)
                count[0] += 1
                route(V.tensor_tensor(totals[:, 1 - src, ahead:TILES], totals[:, src, ahead:TILES],
                                      totals[:, src, 0:TILES - ahead], ALU.add))
                src, ahead = 1 - src, 2 * ahead
            inclusive = totals[:, src]
            route(V.tensor_tensor(over[:, :, :], inclusive[:, TILES - 1, :].unsqueeze(2).broadcast_to([P, E, TILES]),
                                  const("tile_starts").unsqueeze(1).broadcast_to([P, E, TILES]), ALU.is_gt))
            route(V.tensor_reduce(tiles_of[:, :], over[:, :, :], AX, ALU.add))
            for name, sums in (("before", starts), ("upto", ends)):
                route(V.tensor_tensor(square[:, :, :], tiles_of[:, :].unsqueeze(1).broadcast_to([P, E, E]),
                                      const(name).rearrange("p (a b) -> p a b", b=E), ALU.mult))
                route(V.tensor_reduce(sums[:, :], square[:, :, :], AX, ALU.add))
            route(V.tensor_tensor(past[:, :, :], const("slot_tiles").unsqueeze(2).broadcast_to([P, SLOT_TILES, E]),
                                  ends[:, :].unsqueeze(1).broadcast_to([P, SLOT_TILES, E]), ALU.is_ge))
            route(V.tensor_reduce(expert_f[:, :], past[:, :, :], AX, ALU.add))
            V.tensor_scalar(expert[:, :], expert_f[:, :], float(E - 1), None, ALU.min).then_inc(experts_ready, 1)
            route(V.tensor_scalar(starts[:, :], starts[:, :], float(P), -1.0, ALU.mult, ALU.add))
            route(V.tensor_tensor(place[:, :, :], by_tile(0), inclusive, ALU.add))
            route(V.tensor_tensor(place[:, :, :], place[:, :, :], by_tile(1), ALU.subtract))
            route(V.tensor_tensor(place[:, :, :], place[:, :, :],
                                  starts[:, :].unsqueeze(1).broadcast_to([P, TILES, E]), ALU.add))
            route(V.tensor_tensor(place[:, :, :], place[:, :, :], onehots[:, :, :], ALU.mult))
            route(V.tensor_reduce(slot_f[:, :], place[:, :, :], AX, ALU.add))
            V.tensor_scalar(slot[:, :], slot_f[:, :], 0.0, float(SLOT_TILES * P - 1), ALU.max, ALU.min)\
                .then_inc(slots_ready, 1)

            def copy_geluT(n, r):
                dve.wait_ge(gelu_mm, n + 1)
                V.tensor_copy(geluT[:, r % 2], bank[:, 4 + r % 2, :]).then_inc(geluT_done, 1)

            def copy_y(k, r, first):
                k, r = k + r // RING, r % RING
                dve.wait_ge(down_mm, k * RING + r + 1)
                if not first:
                    dve.wait_ge(y_stored[r], 16 * k)
                V.tensor_copy(y_tile[:, r, :], bank[:, 6 + r % 2, 0:P]).then_inc(y_done, 1)

            for n in range(2 * RING):
                copy_geluT(n, n)
                if n >= 1:
                    copy_y(0, n - 1, n <= RING)
            with dve.Fori(2, SLOT_TILES // RING) as k:
                for r in range(RING):
                    copy_geluT(k * RING + r, r)
                    copy_y(k, r - 1, False)
            copy_y(0, SLOT_TILES - 1, False)

            dve.wait_ge(residual_landed, 32)
            for b in range(B):
                dve.wait_ge(gathered[b], 16 * NT)
                got = y_rows[b]
                V.tensor_tensor(got[:, :, :], got[:, :, :], gate_b_rows[:, b, :].unsqueeze(1).broadcast_to([P, NT, P]),
                                ALU.mult).then_inc(final_step, 1)
                dve.wait_ge(final_step, b + 1)
                V.tensor_tensor(got[:, :, :], got[:, :, :], residual_in[:, b * NT:(b + 1) * NT, :], ALU.add)\
                    .then_inc(row_done, 1)


def kernel(**inputs):
    import concourse.bacc as bacc
    from concourse.bass_utils import run_bass_kernel_spmd

    g = {k: np.ascontiguousarray(v) for k, v in inputs.items()}
    x = g["L0_attn_x"]
    arrays = {"x": x, "table": constants(x.shape[1]), "cT": np.ascontiguousarray(g["L0_c"].T), "wmod": g["L0_wmod"],
              "ln_cols": np.ascontiguousarray(np.stack([g[k] for k in (
                  "L0_attn_ln_w", "L0_attn_ln_b", "L0_ffn_ln1_w", "L0_ffn_ln1_b", "L0_ffn_ln2_w",
                  "L0_ffn_ln2_b")], axis=1))}
    for k in ("Wq", "Wk", "Wv", "Wo", "Wg1", "Wg2"):
        arrays[k] = g["L0_attn_" + k]
    for k in ("w_qkv", "w_proj", "gate_w", "gate_b", "w1", "w2"):
        arrays[k] = g["L0_ffn_" + k]
    nc = bacc.Bacc("TRN2", target_bir_lowering=False, num_devices=1)
    aps = {k: nc.dram_tensor("in_" + k, v.shape, F32, kind="ExternalInput").ap() for k, v in arrays.items()}
    out = nc.dram_tensor("out_0", x.shape, F32, kind="ExternalOutput").ap()
    scratch = nc.dram_tensor("modulation", (x.shape[0], 6 * P), F32).ap()
    residual, z_rows = (nc.dram_tensor(n, x.shape, F32).ap() for n in ("residual", "z_rows"))
    z_slots, y_slots = (nc.dram_tensor(n, (SLOT_TILES * P, P), F32).ap() for n in ("z_slots", "y_slots"))
    build(nc, aps, out, scratch, residual, z_rows, z_slots, y_slots)
    r = run_bass_kernel_spmd(nc, [{"in_" + k: v for k, v in arrays.items()}], core_ids=[0])
    return r.results[0]["out_0"]
```

```python
from contextlib import ExitStack

import numpy as np

import concourse.bass as bass
from concourse import mybir

F32 = mybir.dt.float32
F32R = mybir.dt.float32r
U32 = mybir.dt.uint32
ALU = mybir.AluOpType
ACT = mybir.ActivationFunctionType
AX = mybir.AxisListType.X

P = 128
HEADS = 16
HD = P // HEADS
E = 8
LN_X, LN_ATTN, LN_X1, LN_H = range(4)
LNS = 4
DVE_STEPS = 72

LAG_S2 = 16 + 8
LAG_PV = 12
EXP_RING = 4
SHIFT = 18
Y_AT = LAG_S2 + LAG_PV + 17
HEAD = 12
P_AT, PROJ_AT, LN2_AT, T2_AT, LOGITS_AT, ROUTE_AT, COUNT_AT = 14, 16, 18, 25, 27, 28, 32
VALUES_AT = 19
CARRY_AT = 33
LN_SLOTS = 4
CHUNK_AT, UNIT_AT, ATTEND_AT = (85, 93, 14, 22), (0, 1, 2, 4, 6), (94, 15, 23, 31)
LN_ATTN_AT, T_ATTN_AT, OUT_AT, X1_AT, LN_X1_AT, LN_H_AT, T_H_AT = 34, 40, 42, 43, 45, 53, 59
KEY_AT = (61, 62, 66, 67, 74, 75, 87, 89)
LN_X_AT, T_X_AT, QKV_AT, GATE_AT, ROPE_AT, T_QK_AT = 58, 65, (67, 68, 69, 70), 72, 74, 80
END = 1000
UNITS = 19


class Stage:

    def __init__(self, steps):
        self.steps, self.at = steps, 0

    def go_on(self, slot):
        while self.at <= slot:
            self.at = next(self.steps, END)


def is_row(row, n):
    return isinstance(row, int) and row == n


EPS = 1e-5
HG = 4
HJ = HEADS // HG
QR = 32

TILES = 32
REGION = (TILES + 1) * P
SLOT_TILES = TILES + E
RING = 8
Z, RESIDUAL, GATE, TOKEN = slice(0, P), slice(P, 2 * P), slice(2 * P, 3 * P), slice(3 * P, 3 * P + 1)
SLOT = 3 * P + 1

TABLE = {}
_at = 0
for _name, _n in (("ident", P), ("causal", P), ("blockdiag", P), ("head_mask", HEADS), ("cos", 4 * HD),
                  ("sin", 4 * HD), ("k_sel", 3), ("q_sel", 3), ("quad_mask", HJ), ("rank", E), ("ones", P),
                  ("tile_starts", TILES), ("slot_tiles", SLOT_TILES), ("upto", E * E), ("tokens", TILES),
                  ("regions", E)):
    TABLE[_name] = (_at, _n)
    _at += _n
TABLE_COLS = _at


def constants(tokens):
    t = np.zeros((P, TABLE_COLS), np.float32)

    def put(name, values):
        a, n = TABLE[name]
        t[:, a:a + n] = np.asarray(values, np.float32).reshape(P, n)

    p = np.arange(P)
    put("ident", np.eye(P))
    put("causal", p[:, None] <= p[None, :])
    put("blockdiag", p[:, None] // HD == p[None, :] // HD)
    put("head_mask", p[:, None] // HD == np.arange(HEADS)[None, :])
    freq = (1.0 / np.float32(10000.0) ** (np.arange(0, HD, 2, dtype=np.float32) / np.float32(HD))).astype(np.float32)
    pos = (np.arange(tokens // P)[None, :, None] * P + p[:, None, None]).astype(np.float32)
    ang = (pos * freq[None, None, :]).astype(np.float32)
    put("cos", 0.5 * np.concatenate([np.cos(ang), np.cos(ang)], -1))
    put("sin", 0.5 * np.concatenate([-np.sin(ang), np.sin(ang)], -1))
    block = p % QR // HD
    put("k_sel", np.stack([np.choose(block, [1, 1, -1, 0]), np.choose(block, [0, 0, 1, 0]),
                           (block == 3) & (p % HD < 2)], -1))
    put("q_sel", np.stack([np.choose(block, [1, -1, 1, 0]), np.choose(block, [0, 1, 0, 0]), 0 * p], -1))
    put("quad_mask", p[:, None] // QR == np.arange(HJ)[None, :])
    put("rank", np.broadcast_to(np.arange(E) - E, (P, E)))
    put("ones", np.ones((P, P)))
    put("tile_starts", np.broadcast_to(P * np.arange(TILES), (P, TILES)))
    put("slot_tiles", np.broadcast_to(np.arange(SLOT_TILES), (P, SLOT_TILES)))
    e = np.arange(E)
    put("upto", np.broadcast_to((e[None, :] <= e[:, None]).reshape(-1), (P, E * E)))
    put("tokens", P * np.arange(TILES)[None, :] + p[:, None])
    put("regions", np.broadcast_to(REGION * e - 1, (P, E)))
    return t


def build(nc, a, out, scratch, slots):
    B, S, D = a["x"].shape
    NT = S // P
    HID = a["w1"].shape[2]
    HT = HID // P
    NQ = HG * HJ * NT
    SCALE = float(1.0 / np.sqrt(HD))
    assert D == P and S == 512 and HT == 4 and NT == 4 and B * NT == TILES and SLOT_TILES % RING == 0

    with ExitStack() as ctx:
        def sb(name, shape, dt=F32):
            return ctx.enter_context(nc.sbuf_tensor(name, shape, dt))

        def sem(name):
            return ctx.enter_context(nc.semaphore(name))

        table = sb("table", [P, TABLE_COLS])

        def const(name):
            s, n = TABLE[name]
            return table[:, s:s + n]

        ident = const("ident")
        attn_w = sb("attn_w", [P, 4 * P])
        attn_wo = sb("attn_wo", [P, P])
        msa_w = sb("msa_w", [P, 3 * P])
        rep_w = sb("rep_w", [P, 2, HG, HJ, 4, HD])
        proj_w = sb("proj_w", [P, P])
        router_w = sb("router_w", [P, E])
        router_b = sb("router_b", [P, E])
        ln_cols = sb("ln_cols", [P, 6])
        minus_half = sb("minus_half", [P, NT])
        cT = sb("cT", [P, B])
        cth = sb("cth", [P, B])
        mod_bc = sb("mod_bc", [P, 3, P])
        all_mod_cols = sb("all_mod_cols", [P, B, 2])
        mod_cols = sb("mod_cols", [P, 2])
        ident_r = sb("ident_r", [P, P], F32R)
        x = sb("x", [P, NT, P])
        stats = sb("stats", [P, NT, 6])
        moments = sb("moments", [P, 3, NT])
        vareps = sb("vareps", [P, NT])
        rstd = sb("rstd", [P, NT])
        norm = sb("norm", [P, NT, P])
        h = sb("h", [P, NT, P])
        hT = sb("hT", [P, S])
        tanh_qk = sb("tanh_qk", [P, NT, 2 * P])
        tanh_gateT = sb("tanh_gateT", [P, S])
        silu_qk = sb("silu_qk", [P, NT, 2 * P])
        after_silu = silu_qk[:, :, :].rearrange("p t n -> p (t n)").rearrange("p (r n) -> p r n", r=2)
        attnT = after_silu[:, 0]
        x1_gated = after_silu[:, 1].rearrange("p (t n) -> p t n", n=P)
        x1_kept = sb("x1_kept", [P, NT, P])
        h_kept = sb("h_kept", [P, NT, P])
        rows = sb("rows", [P, NT, SLOT])
        y = sb("y", [P, NT, P])
        pT = sb("pT", [P, S])
        rot = sb("rot", [P, NT, 2 * P])
        v = sb("v", [P, NT, P])
        v_heads = sb("v_heads", [P, NT, HG, HJ * (QR + HD)])
        qT = sb("qT", [P, S])
        kT = sb("kT", [P, S])
        exps = sb("exps", [P, EXP_RING, HJ, S])
        wide = exps[:, :, :, :].rearrange("p a b c -> p (a b c)")
        wmod = wide[:, 0:6 * P]
        w1 = wide[:, 0:E * HID].rearrange("p (e n) -> p e n", e=E)
        w2 = wide[:, E * HID:2 * E * HID].rearrange("p (e t n) -> p e t n", e=E, t=HT)
        q_blocks = sb("q_blocks", [P, 2, HEADS, P])
        spare = q_blocks[:, :, :, :].rearrange("p c h n -> p (c h n)")
        scores_m = sb("scores_m", [P, 2, 4, 4, P])
        state = sb("state", [P, 3, P])
        gate1_wT, gate2_w = (spare[0:HD, n * P:(n + 1) * P] for n in (12, 13))
        mod, modt = (spare[0:B, n * 6 * P:(n + 1) * 6 * P] for n in range(2))
        x1 = sb("x1", [P, NT, P])
        vones = sb("vones", [P, NT, HEADS, QR])
        rounded = sb("rounded", [P, 2, S], F32R)
        kq_parts = sb("kq_parts", [P, 2 * HG, S], F32R)
        q_quads = sb("q_quads", [P, HG, HJ, S], F32R)
        negmax = sb("negmax", [P, HG, HJ, NT])
        shift = sb("shift", [P, HG, NT, HJ, 2], F32R)
        shiftT = sb("shiftT", [2 * HJ, 2, S], F32R)
        yT = sb("yT", [P, HG, S])
        pauses = sb("pauses", [P, 2])
        recip = sb("recip", [P, NT, HEADS])
        logits = sb("logits", [P, NT, E])
        best = sb("best", [P, NT])
        onehot = sb("onehot", [P, NT, E])
        cum = sb("cum", [P, NT + 1, E])
        place = sb("place", [P, NT, E])
        slot_f = sb("slot_f", [P, NT])
        slot = sb("slot", [P, NT], U32)
        after_scores = scores_m[:, 0].rearrange("p a b c -> p (a b c)")
        used = [0]

        def take(*shape, dt=F32):
            n = int(np.prod(shape))
            part = after_scores[:, used[0]:used[0] + n]
            used[0] += n
            assert used[0] <= HEADS * P
            if dt != F32:
                part = part.bitcast(dt)
            return part if len(shape) == 1 else part.rearrange(
                {2: "p (a b) -> p a b", 3: "p (a b c) -> p a b c"}[len(shape)],
                **dict(zip("abc"[1:len(shape)], shape[1:])))

        counts = take(E)
        over = take(E, TILES)
        tiles_of = take(E)
        square = take(E, E)
        ends = take(E)
        past = take(SLOT_TILES, E)
        past_ends = take(SLOT_TILES, E)
        first = take(SLOT_TILES)
        expert_f = take(SLOT_TILES)
        region = take(SLOT_TILES)
        expert = sb("expert", [P, SLOT_TILES], U32)
        tile_at = sb("tile_at", [P, SLOT_TILES], U32)
        pads_at = sb("pads_at", [P, E], U32)
        zT = vones[:, :, :, :].rearrange("p a b c -> p (a b c)")[:, 0:2 * P].rearrange("p (a b) -> p a b", b=P)
        y_tile = x
        w1_tile = after_silu
        z_in = spare[:, 0:RING * SLOT].rearrange("p (r n) -> p r n", n=SLOT)
        geluT = yT[:, 0:2]
        pads = spare[:, RING * SLOT:(RING + 1) * SLOT]

        bank = ctx.enter_context(nc.psum_tensor("bank", [P, 8, S], F32))

        c_loaded = sem("c_loaded")
        loaded = sem("loaded")
        gate_w_mm = sem("gate_w_mm")
        prepared = sem("prepared")
        zeroed = sem("zeroed")
        silu_c = sem("silu_c")
        mod_mm = sem("mod_mm")
        mod_step = sem("mod_step")
        mod_ready = sem("mod_ready")
        mod_stored = sem("mod_stored")
        paused = [sem(f"paused{n}") for n in range(2)]
        x_landed = sem("x_landed")
        mod_landed = sem("mod_landed")
        cols_landed = sem("cols_landed")
        var_ready = sem("var_ready")
        rstd_ready = sem("rstd_ready")
        norm_ready = sem("norm_ready")
        pool_step = sem("pool_step")
        h_ready = sem("h_ready")
        transposed = sem("transposed")
        hT_ready = sem("hT_ready")
        crossed = sem("crossed")
        qkv_mm = sem("qkv_mm")
        tanh_ready = sem("tanh_ready")
        gate_mm = sem("gate_mm")
        gate_ready = sem("gate_ready")
        attn_transposed = sem("attn_transposed")
        silu_ready = sem("silu_ready")
        rot_ready = sem("rot_ready")
        q_transposed = sem("q_transposed")
        k_transposed = sem("k_transposed")
        qT_ready = sem("qT_ready")
        kT_ready = sem("kT_ready")
        blocks_ready = sem("blocks_ready")
        unit_mm = sem("unit_mm")
        unit_taken = sem("unit_taken")
        state_ready = sem("state_ready")
        attn_mm = sem("attn_mm")
        gated = sem("gated")
        out_mm = sem("out_mm")
        x1_ready = sem("x1_ready")
        carried = sem("carried")
        vproj_mm = sem("vproj_mm")
        vones_ready = sem("vones_ready")
        qkproj_mm = sem("qkproj_mm")
        rounded_ready = sem("rounded_ready")
        parts_ready = sem("parts_ready")
        quads_ready = sem("quads_ready")
        max_mm = sem("max_mm")
        max_taken = sem("max_taken")
        shift_ready = sem("shift_ready")
        shift_mm = sem("shift_mm")
        shiftT_ready = sem("shiftT_ready")
        shift_landed = [sem(f"shift_landed{n}") for n in range(2)]
        s2_mm = sem("s2_mm")
        exp_ready = sem("exp_ready")
        pv_mm = sem("pv_mm")
        yT_ready = sem("yT_ready")
        y_transposed = sem("y_transposed")
        y_ready = sem("y_ready")
        p_transposed = sem("p_transposed")
        pT_ready = sem("pT_ready")
        proj_mm = sem("proj_mm")
        x2_ready = sem("x2_ready")
        var2_ready = sem("var2_ready")
        rstd2_ready = sem("rstd2_ready")
        norm2_ready = sem("norm2_ready")
        logits_mm = sem("logits_mm")
        routed = sem("routed")
        kept_step = sem("kept_step")
        kept = sem("kept")
        gb_landed = sem("gb_landed")
        counted = sem("counted")
        counts_taken = sem("counts_taken")
        slots_ready = sem("slots_ready")
        scattered = sem("scattered")
        dve_step = sem("dve_step")
        cum_ready = sem("cum_ready")
        route_step = sem("route_step")
        pads_ready = sem("pads_ready")
        pads_at_ready = sem("pads_at_ready")
        padded = sem("padded")
        padded_too = sem("padded_too")
        experts_ready = sem("experts_ready")
        w_loaded = sem("w_loaded")
        z_landed = [sem(f"z_landed{r}") for r in range(RING)]
        z_mm = sem("z_mm")
        zT_done = sem("zT_done")
        w1_copied = sem("w1_copied")
        up_mm = sem("up_mm")
        gelu_done = sem("gelu_done")
        down_mm = sem("down_mm")
        y_scaled = sem("y_scaled")
        y_done = sem("y_done")
        out_stored = [sem(f"out_stored{r}") for r in range(RING)]

        N_LOADS = 12
        SA, CA, GA, SB, CB, GB = range(6)
        PREPARED = 1 + 2 * HG + 1
        SLOTS = NQ + LAG_S2 + LAG_PV
        KEYS_67 = 6

        def key_bank(r):
            return 6 + r % 2 if r < KEYS_67 else 5

        def max_tile(i, following, s):
            if i is not None and s < NQ:
                return i, s
            if following is not None and s >= SLOTS - HEAD:
                return following, s - (SLOTS - HEAD)
            return None, None

        out_rows = out.rearrange("b s d -> (b s) d")
        block = ctx.enter_context(nc.Block())

        @block.sync
        def _(sp):
            def load(dst, src):
                sp.dma_start(dst, src).then_inc(loaded, 16)

            sp.dma_start(cT[:, :], a["cT"]).then_inc(c_loaded, 16)
            sp.dma_start(wmod, a["wmod"]).then_inc(c_loaded, 16)

            def load_x(row):
                sp.dma_start(x[:, :, :], a["x"][bass.ds(row, 1)].rearrange("a (t p) d -> p (a t) d", p=P))\
                    .then_inc(x_landed, 16)

            def mod_rows(row, first, count):
                return scratch[bass.ds(row, 1), first * P:(first + count) * P]

            def load_mod(row):
                sp.dma_start(mod_bc[:, :, :], mod_rows(row, GA, 3).rearrange("a (m d) -> a m d", d=P)
                             .broadcast_to([P, 3, P])).then_inc(mod_landed, 16)

            def load_mod_cols(row):
                sp.dma_start(mod_cols[:, :], all_mod_cols[:, bass.ds(row, 1), :].rearrange("p a n -> p (a n)"))\
                    .then_inc(cols_landed, 16)

            def load_gb(row):
                sp.dma_start(rows[:, :, GATE], mod_rows(row, GB, 1).unsqueeze(1).broadcast_to([P, NT, P]))\
                    .then_inc(gb_landed, 16)

            load_x(0)
            load(table[:, :], a["table"])
            load(gate1_wT[:, :], a["Wg1T"])
            load(gate2_w[:, :], a["Wg2"])
            load(attn_w[:, 0:P], a["Wq"])
            load(attn_w[:, P:2 * P], a["Wk"])
            load(attn_w[:, 2 * P:3 * P], a["Wv"])
            load(msa_w[:, :], a["w_qkv"])
            load(ln_cols[:, :], a["ln_cols"])
            load(attn_wo[:, :], a["Wo"])
            load(proj_w[:, :], a["w_proj"])
            load(router_w[:, :], a["gate_w"])
            load(router_b[:, :], a["gate_b"].unsqueeze(0).broadcast_to([P, E]))
            sp.wait_ge(mod_ready, 1)
            load_mod_cols(0)
            sp.dma_start(scratch, mod[:, :]).then_inc(mod_stored, 16)
            sp.wait_ge(mod_stored, 16)

            def next_x(row):
                sp.wait_ge(x1_ready, row)
                load_x(row)

            def next_mod(row):
                sp.wait_ge(h_ready, row)
                load_mod_cols(row)
                load_mod(row)

            def softmax_row(i, has_before, has_inputs):
                for g in range(HG):
                    if g == 2 and has_before:
                        sp.wait_ge(scattered, 16 * NT * i)
                        load_gb(i)
                    if g == 2 and has_inputs:
                        next_x(i + 2)
                    if g == 3 and has_inputs:
                        next_mod(i + 2)
                    sp.wait_ge(shiftT_ready, i * HG + g + 1)
                    for j in range(HJ):
                        r = QR * j + 3 * HD
                        sp.dma_start(q_quads[r:r + 2, g, j, :].bitcast(F32),
                                     shiftT[2 * j:2 * j + 2, g % 2, :].bitcast(F32)).then_inc(shift_landed[g % 2], 16)

            load_mod(0)
            load_gb(0)
            next_x(1)
            next_mod(1)
            softmax_row(0, False, True)
            with sp.Fori(1, B - 2) as i:
                softmax_row(i, True, True)
            softmax_row(B - 2, True, False)
            softmax_row(B - 1, True, False)
            sp.wait_ge(yT_ready, HG * B)
            sp.dma_start(w1, a["w1"].rearrange("e p n -> p e n")).then_inc(w_loaded, 16)
            sp.dma_start(w2, a["w2"].rearrange("e (t p) n -> p e t n", p=P)).then_inc(w_loaded, 16)
            sp.wait_ge(pads_ready, 2)
            sp.dma_start(slots[E * REGION:E * REGION + P, :], pads).then_inc(padded, 16)
            sp.wait_ge(pads_at_ready, 1)
            for e in range(0, E, 2):
                at = sp.value_load(pads_at[0:1, e:e + 1], min_val=0, max_val=E * REGION)
                sp.dma_start(slots[bass.ds(at, P), :], pads).then_inc(padded, 16)
            sp.wait_ge(scattered, 16 * TILES)
            sp.wait_ge(padded, 16 * (E // 2 + 1))
            sp.wait_ge(padded_too, 16 * E // 2)
            sp.wait_ge(experts_ready, 1)

            def load_z(n, r):
                at = sp.value_load(tile_at[0:1, bass.ds(n, 1)], min_val=0, max_val=E * REGION)
                sp.dma_start(z_in[:, r, :], slots[bass.ds(at, P), :]).then_inc(z_landed[r], 16)

            for r in range(RING):
                load_z(r, r)
            with sp.Fori(1, SLOT_TILES // RING) as k:
                for r in range(RING):
                    sp.wait_ge(out_stored[r], 16 * k)
                    load_z(k * RING + r, r)
            for r in range(RING):
                sp.wait_ge(out_stored[r], 16 * SLOT_TILES // RING)

        @block.gpsimd
        def _(pool):
            nc.gpsimd.memset(minus_half[:, :], -0.5).then_inc(zeroed, 1)
            nc.gpsimd.memset(v_heads[:, :, :, :].rearrange("p a b c -> p (a b c)"), 0.0).then_inc(zeroed, 1)
            nc.gpsimd.memset(rep_w[:, :, :, :, :, :].rearrange("p a b c d e -> p (a b c d e)"), 0.0).then_inc(zeroed, 1)
            nc.gpsimd.memset(vones[:, :, :, :].rearrange("p a b c -> p (a b c)"), 0.0).then_inc(zeroed, 1)
            pool.wait_ge(zeroed, 4)
            nc.gpsimd.memset(vones[:, :, :, HD:HD + 1].rearrange("p a b c -> p (a b c)"), 1.0).then_inc(zeroed, 1)

            nc.gpsimd.memset(pauses[:, :], 0.0).then_inc(paused[0], 1)
            pool.wait_ge(paused[0], 1)
            nc.gpsimd.memset(pauses[:, :], 0.0).then_inc(paused[1], 1)

            def pause(k, n):
                pool.wait_ge(paused[k], n + 1)
                nc.gpsimd.tensor_tensor(pauses[:, k:k + 1], minus_half[:, 0:1], minus_half[:, 1:2], ALU.mult)                    .then_inc(paused[k], 1)

            def rsqrt(ready, done, count):
                pool.wait_ge(ready, count)
                nc.gpsimd.tensor_tensor(rstd[:, :], vareps[:, :], minus_half[:, :], ALU.pow).then_inc(done, 1)

            def query_blocks(row, c):
                if c < 2:
                    pool.wait_ge(qT_ready, row + 1)
                else:
                    pool.wait_ge(unit_mm, row * UNITS + 5 * (c - 1))
                nc.gpsimd.tensor_tensor(q_blocks[:, c % 2], qT[:, c * P:(c + 1) * P].unsqueeze(1)
                                        .broadcast_to([P, HEADS, P]),
                                        const("head_mask").unsqueeze(2).broadcast_to([P, HEADS, P]), ALU.mult)\
                    .then_inc(blocks_ready, 1)

            def modulate(row):
                pool.wait_ge(norm_ready, row * LNS + LN_X1 + 1)
                pool.wait_ge(mod_landed, 16 * row + 16)
                if not is_row(row, 0):
                    pool.wait_ge(carried, 2 * row)
                nc.gpsimd.tensor_tensor(h[:, :, :], norm[:, :, :],
                                        mod_bc[:, CB - GA, :].unsqueeze(1).broadcast_to([P, NT, P]), ALU.mult)\
                    .then_inc(pool_step, 1)
                pool.wait_ge(pool_step, row + 1)
                nc.gpsimd.tensor_tensor(h[:, :, :], h[:, :, :],
                                        mod_bc[:, SB - GA, :].unsqueeze(1).broadcast_to([P, NT, P]), ALU.add)\
                    .then_inc(h_ready, 1)

            def query_quads(row, g):
                pool.wait_ge(parts_ready, row * 2 * HG + 2 * g + 2)
                nc.gpsimd.tensor_tensor(q_quads[:, g], kq_parts[:, 2 * g + 1, :].bitcast(F32).unsqueeze(1)
                                        .broadcast_to([P, HJ, S]),
                                        const("quad_mask").unsqueeze(2).broadcast_to([P, HJ, S]), ALU.mult)\
                    .then_inc(quads_ready, 1)

            def cross(row):
                heads = silu_qk[:, :, :].rearrange("p t (h d) -> p t h d", d=HD)
                crosses = tanh_qk[:, :, :].rearrange("p t (h d) -> p t h d", d=HD)
                sin = const("sin").rearrange("p (t d) -> p t d", d=HD).unsqueeze(2)
                hd2 = HD // 2
                pool.wait_ge(silu_ready, row * NT + NT)
                for d0, d1 in ((0, hd2), (hd2, 0)):
                    nc.gpsimd.tensor_tensor(crosses[:, :, :, d0:d0 + hd2], heads[:, :, :, d1:d1 + hd2],
                                            sin[:, :, :, d0:d0 + hd2].broadcast_to([P, NT, 2 * HEADS, hd2]), ALU.mult)\
                        .then_inc(crossed, 1)

            def finish(row):
                pool.wait_ge(norm2_ready, row + 1)
                pool.wait_ge(gb_landed, 16 * row + 16)
                nc.gpsimd.tensor_tensor(rows[:, :, RESIDUAL], h_kept[:, :, :], rows[:, :, GATE], ALU.mult)\
                    .then_inc(kept_step, 1)
                pool.wait_ge(kept_step, row + 1)
                nc.gpsimd.tensor_tensor(rows[:, :, RESIDUAL], rows[:, :, RESIDUAL], x1_kept[:, :, :], ALU.add)\
                    .then_inc(kept, 1)

            def scatter(row):
                pool.wait_ge(kept, row + 1)
                pool.wait_ge(slots_ready, row + 1)
                pause(0, row)
                for t in range(NT):
                    pool.indirect_dma_start(slots, bass.IndirectOffsetOnAxis(ap=slot[:, t:t + 1], axis=0),
                                            rows[:, t, :], None).then_inc(scattered, 16)

            def softmax_row(before, after, ahead):
                if after is not None:
                    query_blocks(after, 3)
                if before is not None:
                    rsqrt(var2_ready, rstd2_ready, before + 1)
                if before is not None:
                    finish(before)
                if after is not None:
                    rsqrt(var_ready, rstd_ready, after * LNS + LN_ATTN + 1)
                if before is not None:
                    scatter(before)
                if after is not None:
                    rsqrt(var_ready, rstd_ready, after * LNS + LN_X1 + 1)
                    modulate(after)
                    rsqrt(var_ready, rstd_ready, after * LNS + LN_H + 1)
                if ahead is not None:
                    rsqrt(var_ready, rstd_ready, ahead * LNS + LN_X + 1)
                if after is not None:
                    query_quads(after, 0)
                    query_quads(after, 1)
                if ahead is not None:
                    cross(ahead)
                if after is not None:
                    query_quads(after, 2)
                if ahead is not None:
                    for c in range(3):
                        query_blocks(ahead, c)
                if after is not None:
                    query_quads(after, 3)

            rsqrt(var_ready, rstd_ready, 1)
            pool.wait_ge(loaded, 16 * N_LOADS)
            cross(0)
            pool.wait_ge(mod_stored, 16)
            for c in range(3):
                query_blocks(0, c)
            softmax_row(None, 0, 1)
            softmax_row(None, 1, 2)
            with pool.Fori(1, B - 2) as i:
                softmax_row(i - 1, i + 1, i + 2)
            softmax_row(B - 3, B - 1, None)
            softmax_row(B - 2, None, None)
            pool.wait_ge(unit_mm, UNITS * B)
            nc.gpsimd.memset(pads, 0.0).then_inc(pads_ready, 1)
            pool.wait_ge(pads_ready, 1)
            nc.gpsimd.memset(pads[:, TOKEN].bitcast(U32), B * S).then_inc(pads_ready, 1)
            softmax_row(B - 1, None, None)

            def scatter_out(n, r):
                pool.wait_ge(y_done, n + 1)
                pause(1, n)
                pool.indirect_dma_start(out_rows, bass.IndirectOffsetOnAxis(ap=z_in[:, r, TOKEN].bitcast(U32), axis=0),
                                        y_tile[:, r % 4, :], None, bounds_check=B * S - 1, oob_is_err=False)\
                    .then_inc(out_stored[r], 16)

            with pool.Fori(0, SLOT_TILES // RING) as k:
                for r in range(RING):
                    scatter_out(k * RING + r, r)

        @block.scalar
        def _(act):
            act.wait_ge(c_loaded, 32)
            nc.scalar.activation(cth[:, :], cT[:, :], ACT.Tanh, scale=0.5).then_inc(silu_c, 1)

            act.wait_ge(loaded, 16 * N_LOADS)

            def copy_T(row, n, dst, b, w, bias):
                act.wait_ge(transposed, row * 3 + n + 1)
                nc.scalar.activation(dst[:, :], bank[:, b, :], ACT.Identity, scale=w, bias=bias).then_inc(hT_ready, 1)

            def inputs(row):
                if is_row(row, 0):
                    act.wait_ge(zeroed, 2)
                yield T_X_AT + 1
                act.wait_ge(cols_landed, 16 * row + 16)
                copy_T(row, 0, pT, 0, mod_cols[:, 1:2], mod_cols[:, 0:1])
                for t in range(NT):
                    yield QKV_AT[t] + 1
                    act.wait_ge(qkv_mm, row * NT + t + 1)
                    nc.scalar.activation(tanh_qk[:, t, :], bank[:, t % 2, 0:2 * P], ACT.Tanh, scale=0.5)
                    nc.scalar.activation(v[:, t, :], bank[:, t % 2, 2 * P:3 * P], ACT.Identity)
                    nc.scalar.activation(v_heads[:, t].rearrange("p q (j n) -> p q j n", j=HJ)[:, :, :, 0:HD], bank[:, t % 2, 2 * P:3 * P].rearrange(
                        "p (q j d) -> p q j d", q=HG, d=HD), ACT.Identity).then_inc(tanh_ready, 1)
                yield GATE_AT + 1
                act.wait_ge(gate_mm, row + 1)
                nc.scalar.activation(tanh_gateT[:, :], bank[:, 0, :], ACT.Tanh, scale=0.5).then_inc(gate_ready, 1)
                yield T_QK_AT + 1
                act.wait_ge(q_transposed, row + 1)
                nc.scalar.activation(qT[:, :], bank[:, 0, :], ACT.Identity).then_inc(qT_ready, 1)
                yield T_QK_AT + 2
                act.wait_ge(k_transposed, row + 1)
                nc.scalar.activation(kT[:, :], bank[:, 1, :], ACT.Identity).then_inc(kT_ready, 1)

            def linear(row):
                yield T_ATTN_AT + 1
                copy_T(row, 1, pT, 7, ln_cols[:, 0:1], ln_cols[:, 1:2])
                yield T_H_AT + 1
                copy_T(row, 2, hT, 7, ln_cols[:, 2:3], ln_cols[:, 3:4])

            def keys(row):
                for r in range(2 * HG):
                    yield KEY_AT[r] + 1
                    act.wait_ge(qkproj_mm, row * 2 * HG + r + 1)
                    if r >= 2:
                        act.wait_ge(parts_ready, row * 2 * HG + r - 1)
                    sel = const(("k_sel", "q_sel")[r % 2])
                    nc.scalar.activation(rounded[:, r % 2, :], bank[:, key_bank(r), :], ACT.Identity,
                                         scale=sel[:, 0:1], bias=sel[:, 2:3]).then_inc(rounded_ready, 1)

            def values(row):
                yield VALUES_AT + 1
                act.wait_ge(vproj_mm, row + 1)
                nc.scalar.activation(vones[:, :, :, 0:HD],
                                     bank[:, 4, :].rearrange("p (t h d) -> p t h d", h=HEADS, d=HD),
                                     ACT.Identity).then_inc(vones_ready, 1)

            def finish(row):
                yield P_AT + 1
                act.wait_ge(p_transposed, row * 2 + 1)
                nc.scalar.activation(pT[:, :], bank[:, 4, :], ACT.Identity).then_inc(pT_ready, 1)
                yield T2_AT + 1
                act.wait_ge(p_transposed, row * 2 + 2)
                nc.scalar.activation(pT[:, :], bank[:, 4, :], ACT.Identity, scale=ln_cols[:, 4:5],
                                     bias=ln_cols[:, 5:6]).then_inc(pT_ready, 1)

            def carry(row, has_before):
                yield CARRY_AT
                if has_before:
                    act.wait_ge(kept, row)
                nc.scalar.activation(h_kept[:, :, :], h[:, :, :], ACT.Identity).then_inc(carried, 1)
                yield CARRY_AT + 2
                nc.scalar.activation(x1_kept[:, :, :], x1[:, :, :], ACT.Identity).then_inc(carried, 1)

            def softmax_row(i, *stages):
                stages = [Stage(steps) for steps in stages]
                for s in range(HEAD, SLOTS):
                    for stage in stages:
                        stage.go_on(s)
                    if i is None:
                        continue
                    if s % 16 == SHIFT % 16 and SHIFT <= s < SHIFT + 16 * HG:
                        g = (s - SHIFT) // 16
                        act.wait_ge(shift_mm, i * HG + g + 1)
                        if g >= 2:
                            act.wait_ge(shift_landed[g % 2], i * 16 * HJ * 2 + 16 * HJ)
                        nc.scalar.activation(shiftT[:, g % 2, :], bank[0:2 * HJ, 5, :], ACT.Identity)\
                            .then_inc(shiftT_ready, 1)
                    m = s - LAG_S2
                    if 0 <= m < NQ:
                        w, j = divmod(m, HJ)
                        act.wait_ge(s2_mm, i * NQ + m + 1)
                        if j == 0 and w >= EXP_RING:
                            act.wait_ge(pv_mm, i * HG * NT + w + 1 - EXP_RING)
                        nc.scalar.activation(exps[:, w % EXP_RING, j, :], bank[:, 2 + m % 2, :], ACT.Exp, scale=SCALE)\
                            .then_inc(exp_ready, 1)
                    if m >= 27 and m % 16 == 11:
                        g = (m - 27) // 16
                        act.wait_ge(pv_mm, i * HG * NT + NT * (g + 1))
                        nc.scalar.activation(yT[:, g, :], bank[:, 4, :], ACT.Identity).then_inc(yT_ready, 1)
                for stage in stages:
                    stage.go_on(END - 1)

            softmax_row(None, inputs(0))
            softmax_row(None, linear(0), inputs(1), keys(0))
            softmax_row(0, values(0), carry(0, False), linear(1), inputs(2), keys(1))
            with act.Fori(1, B - 2) as i:
                softmax_row(i, finish(i - 1), values(i), carry(i, True), linear(i + 1), inputs(i + 2), keys(i + 1))
            softmax_row(B - 2, finish(B - 3), values(B - 2), carry(B - 2, True), linear(B - 1), keys(B - 1))
            softmax_row(B - 1, finish(B - 2), values(B - 1), carry(B - 1, True))
            softmax_row(None, finish(B - 1))

            act.wait_ge(pads_ready, 2)
            act.wait_ge(pads_at_ready, 1)
            for e in range(1, E, 2):
                at = act.value_load(pads_at[0:1, e:e + 1], min_val=0, max_val=E * REGION)
                act.dma_start(slots[bass.ds(at, P), :], pads).then_inc(padded_too, 16)

            def copy_z(n, r):
                act.wait_ge(z_mm, n + 1)
                nc.scalar.activation(zT[:, r % 2, :], bank[:, r % 2, 0:P], ACT.Identity, scale=ln_cols[:, 4:5],
                                     bias=ln_cols[:, 5:6]).then_inc(zT_done, 1)

            def activate(n, r):
                act.wait_ge(up_mm, n + 1)
                nc.scalar.activation(geluT[:, r % 2], bank[:, 2 + r % 2, :], ACT.Gelu_apprx_tanh)\
                    .then_inc(gelu_done, 1)

            copy_z(0, 0)
            with act.Fori(0, SLOT_TILES // RING - 1) as k:
                for r in range(RING):
                    copy_z(k * RING + r + 1, r + 1)
                    activate(k * RING + r, r)
            for n in range(SLOT_TILES - RING, SLOT_TILES):
                if n + 1 < SLOT_TILES:
                    copy_z(n + 1, n + 1)
                activate(n, n)

        @block.tensor
        def _(pe):
            mm = nc.tensor.matmul
            pe.wait_ge(silu_c, 2)
            mm(bank[0:B, 0, :], cth[:, :], wmod[:, 0:S], start=True, stop=True)
            for n in range(2):
                mm(bank[:, 3, n * B:(n + 1) * B], wmod[:, n * P:(n + 1) * P], cth[:, :], start=True, stop=True)
            mm(bank[0:B, 1, 0:2 * P], cth[:, :], wmod[:, S:6 * P], start=True, stop=True).then_inc(mod_mm, 1)
            pe.wait_ge(loaded, 16 * N_LOADS)
            mm(bank[:, 2, 0:P], gate1_wT[:, :], gate2_w[:, :], start=True, stop=True).then_inc(gate_w_mm, 1)

            def tile(T, t):
                return T[:, t * P:(t + 1) * P]

            def transpose_tiles(b, src, signal):
                for t in range(NT):
                    last = nc.tensor.transpose(tile(bank[:, b, :], t), src(t), ident)
                last.then_inc(signal, 1)

            def unit(row, c, n):
                u = 5 * c + (n if c < NT - 1 or n == 0 else n - 1)
                if u >= 2:
                    pe.wait_ge(unit_taken, row * UNITS + u - 1)
                elif not is_row(row, 0):
                    pe.wait_ge(parts_ready, (row - 1) * 2 * HG + KEYS_67)
                if n == 1:
                    last = mm(bank[:, 6 + u % 2, 0:P], rot[:, c, P:2 * P], v[:, c, :], start=True, stop=True)
                else:
                    if n == 0:
                        pe.wait_ge(blocks_ready, row * NT + c + 1)
                    q = max(n - 1, 0)
                    last = mm(bank[:, 6 + u % 2, :].rearrange("p (h n) -> p h n", n=P), tile(kT, c),
                              q_blocks[:, c % 2].rearrange("p (q j) n -> p j q n", j=4)[:, q], start=True, stop=True)
                last.then_inc(unit_mm, 1)

            def attend(row, c, core):
                if c >= 1:
                    pe.wait_ge(gated, row * NT + c)
                elif not is_row(row, 0):
                    pe.wait_ge(parts_ready, row * 2 * HG)
                if core is not None and c == 2:
                    pe.wait_ge(shiftT_ready, core * HG + 1)
                if c >= 2:
                    pe.wait_ge(state_ready, row * (NT - 2) + c - 1)
                pe.wait_ge(unit_taken, row * UNITS + min(5 * (c + 1), UNITS))
                if c >= 1:
                    mm(bank[:, 5, 0:P], state[:, c - 1, :], tile(qT, c), start=True, stop=False,
                       skip_group_check=True)
                for n in range(4):
                    for q in range(HG):
                        last = mm(bank[QR * q:QR * (q + 1), 5, 0:P], v_heads[:, c, q, QR * n:QR * (n + 1)],
                                  scores_m[:, c % 2, n, q, :],
                                  start=c == 0 and n == 0, stop=n == 3, skip_group_check=True)
                last.then_inc(attn_mm, 1)

            def chunk(row, c):
                for n in range(5):
                    if n != 1 or c < NT - 1:
                        yield CHUNK_AT[c] + UNIT_AT[n]
                        unit(row, c, n)

            def inputs(row, core):
                yield T_X_AT
                pe.wait_ge(norm_ready, row * LNS + LN_X + 1)
                if core is not None:
                    pe.wait_ge(max_taken, core * NQ + NQ)
                elif row:
                    pe.wait_ge(kT_ready, row)
                transpose_tiles(0, lambda t: norm[:, t, :], transposed)
                for t in range(NT):
                    yield QKV_AT[t]
                    if t == 0:
                        pe.wait_ge(hT_ready, row * 3 + 1)
                    if t >= 2:
                        pe.wait_ge(silu_ready, row * NT + t - 1)
                    mm(bank[:, t % 2, 0:3 * P], tile(pT, t), attn_w[:, 0:3 * P], start=True, stop=True)\
                        .then_inc(qkv_mm, 1)
                yield GATE_AT
                if is_row(row, 0):
                    pe.wait_ge(prepared, PREPARED)
                    pe.wait_ge(zeroed, 5)
                pe.wait_ge(silu_ready, row * NT + NT - 1)
                mm(bank[:, 0, :], attn_w[:, 3 * P:4 * P], pT[:, :], start=True, stop=True).then_inc(gate_mm, 1)
                yield T_QK_AT
                pe.wait_ge(rot_ready, row + 1)
                pe.wait_ge(gate_ready, row + 1)
                transpose_tiles(0, lambda t: rot[:, t, 0:P], q_transposed)
                yield T_QK_AT + 1
                transpose_tiles(1, lambda t: rot[:, t, P:2 * P], k_transposed)
                steps = sorted([(CHUNK_AT[c] + UNIT_AT[n], c, n) for c in range(2) for n in range(5)] +
                               [(ATTEND_AT[0], 0, None)], key=lambda step: step[:2])
                for at, c, n in steps:
                    yield at
                    if n is None:
                        attend(row, 0, None)
                    else:
                        if c == n == 0:
                            pe.wait_ge(kT_ready, row + 1)
                        unit(row, c, n)

            def linear(row, core):
                for c in range(1, NT):
                    if c >= 2:
                        yield from chunk(row, c)
                    yield ATTEND_AT[c]
                    attend(row, c, core)
                yield LN_ATTN_AT - 1
                pe.wait_ge(gated, row * NT + NT)
                transpose_tiles(6, lambda t: tile(attnT, t), attn_transposed)
                yield T_ATTN_AT
                pe.wait_ge(norm_ready, row * LNS + LN_ATTN + 1)
                transpose_tiles(7, lambda t: norm[:, t, :], transposed)
                yield OUT_AT
                pe.wait_ge(hT_ready, row * 3 + 2)
                for t in range(NT):
                    last = mm(tile(bank[:, 6, :], t), tile(pT, t), attn_wo[:, :], start=True, stop=True)
                last.then_inc(out_mm, 1)
                yield T_H_AT
                pe.wait_ge(norm_ready, row * LNS + LN_H + 1)
                transpose_tiles(7, lambda t: norm[:, t, :], transposed)

            def keys(row):
                for r in range(2 * HG):
                    yield KEY_AT[r]
                    if r == 0:
                        pe.wait_ge(hT_ready, row * 3 + 3)
                    if r >= 2:
                        pe.wait_ge(parts_ready, row * 2 * HG + r - (r <= KEYS_67))
                    if r == KEYS_67:
                        if is_row(row, 0):
                            pe.wait_ge(gated, NT)
                        else:
                            pe.wait_ge(y_ready, (row - 1) * HG + HG - 1)
                    mm(bank[:, key_bank(r), :], rep_w[:, 1 - r % 2, r // 2].rearrange("p j c d -> p (j c d)"),
                       hT[:, :], start=True, stop=True).then_inc(qkproj_mm, 1)

            def values(row, has_before):
                yield VALUES_AT
                pe.wait_ge(hT_ready, row * 3 + 3)
                if has_before:
                    pe.wait_ge(x2_ready, row)
                for t in range(NT):
                    last = mm(tile(bank[:, 4, :], t), tile(hT, t), msa_w[:, 2 * P:3 * P], start=True, stop=True)
                last.then_inc(vproj_mm, 1)

            def transpose_y(row, g, b):
                pe.wait_ge(yT_ready, row * HG + g + 1)
                for t in range(NT):
                    last = nc.tensor.transpose(tile(bank[:, b, :], t), tile(yT[:, g], t), ident)
                last.then_inc(y_transposed, 1)

            def outputs(row):
                for g in range(HG - 1):
                    yield Y_AT + 16 * g
                    pe.wait_ge(shiftT_ready, row * HG + min(g + 3, HG))
                    if g >= 1:
                        pe.wait_ge(y_ready, row * HG + g)
                    transpose_y(row, g, 5)

            def finish(row, has_next):
                yield HEAD
                transpose_y(row, HG - 1, 4)
                yield P_AT
                pe.wait_ge(y_ready, row * HG + HG)
                transpose_tiles(4, lambda t: y[:, t, :], p_transposed)
                yield PROJ_AT
                pe.wait_ge(pT_ready, row * 2 + 1)
                for t in range(NT):
                    last = mm(tile(bank[:, 4, :], t), tile(pT, t), proj_w[:, :], start=True, stop=True)
                last.then_inc(proj_mm, 1)
                yield T2_AT
                pe.wait_ge(norm2_ready, row + 1)
                if has_next:
                    pe.wait_ge(vones_ready, row + 2)
                transpose_tiles(4, lambda t: rows[:, t, Z], p_transposed)
                yield LOGITS_AT
                pe.wait_ge(pT_ready, row * 2 + 2)
                for t in range(NT):
                    last = mm(bank[:, 4, t * E:(t + 1) * E], tile(pT, t), router_w[:, :], start=True, stop=True)
                last.then_inc(logits_mm, 1)
                yield COUNT_AT
                pe.wait_ge(routed, row + 1)
                flat = onehot[:, :, :].rearrange("p t e -> p (t e)")
                mm(bank[:, 4, P:P + NT * E], const("causal"), flat, start=True, stop=True)
                mm(bank[:, 4, 2 * P:2 * P + NT * E], const("ones"), flat, start=True, stop=True).then_inc(counted, 1)

            def k_part(g):
                return kq_parts[:, 2 * g, :]

            def max_scores(i, a, has_next):
                g, j, t = a // (HJ * NT), a // NT % HJ, a % NT
                if j == t == 0:
                    pe.wait_ge(quads_ready, i * HG + g + 1)
                if a >= 2:
                    pe.wait_ge(max_taken, i * NQ + a - 1)
                elif has_next:
                    pe.wait_ge((qT_ready, kT_ready)[a], i + 2)
                else:
                    pe.wait_ge(max_taken, i * NQ)
                mm(bank[:, a % 2, :], tile(q_quads[:, g, j], t), k_part(g), start=True, stop=True)\
                    .then_inc(max_mm, 1)

            def shift_rows(i, g, has_next):
                pe.wait_ge(shift_ready, i * HG + g + 1)
                if g >= 1:
                    pe.wait_ge(shiftT_ready, i * HG + g)
                if has_next and g < 2:
                    pe.wait_ge(gated, (i + 1) * NT + (2, NT)[g])
                if g == HG - 1:
                    pe.wait_ge(y_ready, i * HG + 1)
                for t in range(NT):
                    last = mm(tile(bank[0:2 * HJ, 5, :], t), shift[:, g, t].rearrange("p j s -> p (j s)"),
                              ident_r[:, :], start=True, stop=True)
                last.then_inc(shift_mm, 1)

            def shifted_scores(i, m):
                g, t, j = m // (NT * HJ), m // HJ % NT, m % HJ
                if m % 16 == 0:
                    pe.wait_ge(shift_landed[g % 2], i * 16 * HJ * 2 + 16 * HJ * (g // 2 + 1))
                if m >= 2:
                    pe.wait_ge(exp_ready, i * NQ + m - 1)
                mm(bank[:, 2 + m % 2, :], tile(k_part(g), t), q_quads[:, g, j],
                   start=True, stop=True).then_inc(s2_mm, 1)

            def weighted_values(i, n, has_before):
                w, j = divmod(n, HJ)
                g, t = divmod(w, NT)
                if j == 0:
                    pe.wait_ge(exp_ready, i * NQ + n + HJ)
                    if g >= 1 and t == 0:
                        pe.wait_ge(yT_ready, i * HG + g)
                    if n == 0:
                        pe.wait_ge(vones_ready, i + 1)
                        if has_before:
                            pe.wait_ge(counts_taken, i)
                last = mm(bank[QR * j:QR * (j + 1), 4, :], vones[:, t, HJ * g + j, :],
                          exps[:, w % EXP_RING, j, :], start=t == 0, stop=t == NT - 1)
                if j == HJ - 1:
                    last.then_inc(pv_mm, 1)

            def softmax_row(i, following, has_before, has_next, has_ahead, *stages):
                stages = [Stage(steps) for steps in stages]
                for s in range(HEAD, SLOTS):
                    row, a = max_tile(i, following, s)
                    if row is not None:
                        max_scores(row, a, has_ahead)
                    for stage in stages:
                        stage.go_on(s)
                    if i is None:
                        continue
                    if s % 16 == SHIFT % 16 and SHIFT <= s < SHIFT + 16 * HG:
                        shift_rows(i, (s - SHIFT) // 16, has_next)
                    if 0 <= s - LAG_S2 < NQ:
                        shifted_scores(i, s - LAG_S2)
                    if 0 <= s - LAG_S2 - LAG_PV:
                        weighted_values(i, s - LAG_S2 - LAG_PV, has_before)
                for stage in stages:
                    stage.go_on(END - 1)

            softmax_row(None, None, False, False, False, inputs(0, None))
            softmax_row(None, 0, False, True, True, linear(0, None), inputs(1, None), keys(0))
            softmax_row(0, 1, False, True, True, values(0, False), linear(1, 0), outputs(0), inputs(2, 0), keys(1))
            with pe.Fori(1, B - 2) as i:
                softmax_row(i, i + 1, True, True, True, finish(i - 1, True), values(i, True), linear(i + 1, i),
                            outputs(i), inputs(i + 2, i), keys(i + 1))
            softmax_row(B - 2, B - 1, True, True, False, finish(B - 3, True), values(B - 2, True),
                        linear(B - 1, B - 2), outputs(B - 2), keys(B - 1))
            softmax_row(B - 1, None, True, False, False, finish(B - 2, True), values(B - 1, True), outputs(B - 1))
            softmax_row(None, None, True, False, False, finish(B - 1, False))

            def transpose_z(k, r):
                k, r = k + r // RING, r % RING
                pe.wait_ge(z_landed[r], 16 * (k + 1))
                nc.tensor.transpose(bank[:, r % 2, 0:P], z_in[:, r, Z], ident).then_inc(z_mm, 1)

            def expert_of(n):
                return pe.value_load(expert[0:1, bass.ds(n, 1)], min_val=0, max_val=E - 1)

            def up(n, r, is_first):
                pe.wait_ge(w1_copied, n + 1)
                pe.wait_ge(zT_done, n + 1)
                if not is_first:
                    pe.wait_ge(gelu_done, n - 1)
                for t in range(HT):
                    last = mm(tile(bank[:, 2 + r % 2, :], t), tile(w1_tile[:, r % 2], t), zT[:, r % 2, :],
                              start=True, stop=True)
                last.then_inc(up_mm, 1)

            def down(n, r, is_first):
                e = expert_of(n)
                pe.wait_ge(gelu_done, n + 1)
                if not is_first:
                    pe.wait_ge(y_done, n - 1)
                for t in range(HT):
                    last = mm(bank[:, 6 + r % 2, 0:P], tile(geluT[:, r % 2], t),
                              w2[:, bass.ds(e, 1), t, :].rearrange("p a n -> p (a n)"),
                              start=t == 0, stop=t == HT - 1)
                last.then_inc(down_mm, 1)

            pe.wait_ge(experts_ready, 2)
            pe.wait_ge(w_loaded, 32)
            transpose_z(0, 0)
            for n in range(RING):
                transpose_z(0, n + 1)
                up(n, n, n < 2)
                if n >= 1:
                    down(n - 1, n - 1, n < 3)
            with pe.Fori(1, SLOT_TILES // RING - 1) as k:
                for r in range(RING):
                    transpose_z(k, r + 1)
                    up(k * RING + r, r, False)
                    down(k * RING + r - 1, r - 1, False)
            for n in range(SLOT_TILES - RING, SLOT_TILES + 1):
                if n + 1 < SLOT_TILES:
                    transpose_z(0, n + 1)
                if n < SLOT_TILES:
                    up(n, n, False)
                down(n - 1, n - 1, False)

        @block.vector
        def _(dve):
            V = nc.vector
            dve.wait_ge(silu_c, 1)
            V.scalar_tensor_tensor(cth[:, :], cth[:, :], 1.0, cT[:, :], ALU.add, ALU.mult).then_inc(silu_c, 1)
            dve.wait_ge(mod_mm, 1)
            V.tensor_scalar(mod[:, 0:S], bank[0:B, 0, :], 0.5, None, ALU.mult).then_inc(mod_step, 1)
            V.tensor_scalar(mod[:, S:6 * P], bank[0:B, 1, 0:2 * P], 0.5, None, ALU.mult).then_inc(mod_step, 1)
            dve.wait_ge(mod_step, 2)
            for n, m in enumerate((1, 4)):
                V.tensor_scalar(mod[:, m * P:(m + 1) * P], mod[:, m * P:(m + 1) * P], 1.0, None, ALU.add)\
                    .then_inc(mod_step, 1)
            for n, m in enumerate((2, 5)):
                V.tensor_scalar(modt[:, m * P:(m + 1) * P], mod[:, m * P:(m + 1) * P], 0.0, 2.0, ALU.is_ge,
                                ALU.mult).then_inc(mod_step, 1)
            for n, m in enumerate((2, 5)):
                gate = mod[:, m * P:(m + 1) * P]
                dve.wait_ge(mod_step, 6 + 3 * n)
                V.scalar_tensor_tensor(gate, gate, -1.0, gate, ALU.mult, ALU.max).then_inc(mod_step, 1)
                dve.wait_ge(mod_step, 7 + 3 * n)
                V.tensor_scalar(gate, gate, 0.25, None, ALU.max).then_inc(mod_step, 1)
                dve.wait_ge(mod_step, 8 + 3 * n)
                V.scalar_tensor_tensor(gate, modt[:, m * P:(m + 1) * P], -1.0, gate, ALU.add, ALU.mult)\
                    .then_inc(mod_step, 1)
            V.tensor_scalar(all_mod_cols[:, :, 0], bank[:, 3, 0:B], 0.5, None, ALU.mult).then_inc(mod_step, 1)
            V.tensor_scalar(all_mod_cols[:, :, 1], bank[:, 3, B:2 * B], 0.5, 1.0, ALU.mult, ALU.add)\
                .then_inc(mod_step, 1)
            dve.wait_ge(mod_step, 14)
            V.memset(y[:, 0, 0:1], 0.0).then_inc(mod_ready, 1)
            steps = [0, 0]

            def step(instruction):
                steps[1] += 1
                instruction.then_inc(dve_step, 1)

            def settle():
                dve.wait_ge(dve_step, steps[0] + steps[1])

            def variances(at, src, eps, signal):
                for t in range(NT):
                    if t == 2:
                        yield at + 1
                    step(V.bn_stats(stats[:, t, :], src[:, t, :]))
                yield at + 2
                settle()
                (mean_e, var_e), (mean_o, var_o) = ((stats[:, :, n], stats[:, :, n + 1]) for n in (1, 4))
                mean, diff, var = (moments[:, n, :] for n in range(3))
                step(V.tensor_tensor(mean, mean_e, mean_o, ALU.add))
                step(V.tensor_tensor(diff, mean_e, mean_o, ALU.subtract))
                step(V.tensor_tensor(var, var_e, var_o, ALU.add))
                settle()
                step(V.tensor_scalar(mean, mean, 0.5, None, ALU.mult))
                step(V.tensor_tensor(diff, diff, diff, ALU.mult))
                step(V.tensor_scalar(var, var, 1.0 / P, eps, ALU.mult, ALU.add))
                settle()
                V.scalar_tensor_tensor(vareps[:, :], diff, 0.25, var, ALU.mult, ALU.add).then_inc(signal, 1)

            def normalize(at, src, rstd_signal, count, signal, dst=norm):
                dve.wait_ge(rstd_signal, count)
                for t in range(NT):
                    if t == 2:
                        yield at + 1
                    last = V.tensor_scalar(dst[:, t, 0:P], src[:, t, :], moments[:, 0, t:t + 1], rstd[:, t:t + 1],
                                           ALU.subtract, ALU.mult)
                last.then_inc(signal, 1)

            def layer_norm(row, n, src, eps, free, count):
                at = (LN_X_AT, LN_ATTN_AT, LN_X1_AT, LN_H_AT)[n]
                yield from variances(at, src, eps, var_ready)
                at += LN_SLOTS
                yield at
                if free is not None:
                    dve.wait_ge(free, count)
                yield from normalize(at, src, rstd_ready, row * LNS + n + 1, norm_ready)

            def tiles(b):
                return bank[:, b, :].rearrange("p (t n) -> p t n", n=P)

            def take_unit(row, c, n):
                u = 5 * c + (n if c < NT - 1 or n == 0 else n - 1)
                dve.wait_ge(unit_mm, row * UNITS + u + 1)
                if n == 1:
                    V.tensor_tensor(state[:, c, :], bank[:, 6 + u % 2, 0:P], const("blockdiag"), ALU.mult)\
                        .then_inc(unit_taken, 1)
                    if c >= 1:
                        dve.wait_ge(unit_taken, row * UNITS + u + 1)
                        V.tensor_tensor(state[:, c, :], state[:, c, :], state[:, c - 1, :], ALU.add)\
                            .then_inc(state_ready, 1)
                    return
                if n == 0 and c >= 2:
                    dve.wait_ge(attn_mm, row * NT + c - 1)
                V.tensor_tensor(scores_m[:, c % 2, max(n - 1, 0)],
                                bank[:, 6 + u % 2, :].rearrange("p (h n) -> p h n", n=P),
                                const("causal").unsqueeze(1).broadcast_to([P, 4, P]), ALU.mult)\
                    .then_inc(unit_taken, 1)

            def chunk(row, c):
                for n in range(5):
                    if n != 1 or c < NT - 1:
                        yield CHUNK_AT[c] + UNIT_AT[n] + 1
                        take_unit(row, c, n)

            def gate(row, c):
                if c == 0:
                    dve.wait_ge(gate_ready, row + 1)
                dve.wait_ge(attn_mm, row * NT + c + 1)
                at = slice(c * P, (c + 1) * P)
                V.scalar_tensor_tensor(attnT[:, at], tanh_gateT[:, at], 1.0, bank[:, 5, 0:P], ALU.add, ALU.mult)\
                    .then_inc(gated, 1)

            def inputs(row):
                yield LN_X_AT
                dve.wait_ge(x_landed, 16 * row + 16)
                yield from layer_norm(row, LN_X, x, EPS, *((None, 0) if is_row(row, 0) else (transposed, 3 * row)))
                for t in range(NT):
                    yield QKV_AT[t] + 2
                    dve.wait_ge(tanh_ready, row * NT + t + 1)
                    V.scalar_tensor_tensor(silu_qk[:, t, :], tanh_qk[:, t, :], 1.0, bank[:, t % 2, 0:2 * P],
                                           ALU.add, ALU.mult).then_inc(silu_ready, 1)
                yield ROPE_AT
                dve.wait_ge(silu_ready, row * NT + NT)
                step(V.tensor_tensor(rot[:, :, :].rearrange("p t (h d) -> p t h d", d=HD),
                                     silu_qk[:, :, :].rearrange("p t (h d) -> p t h d", d=HD),
                                     const("cos").rearrange("p (t d) -> p t d", d=HD).unsqueeze(2)
                                     .broadcast_to([P, NT, 2 * HEADS, HD]), ALU.mult))
                yield ROPE_AT + 4
                settle()
                dve.wait_ge(crossed, 2 * row + 2)
                V.tensor_tensor(rot[:, :, :], rot[:, :, :], tanh_qk[:, :, :], ALU.add).then_inc(rot_ready, 1)
                steps = sorted([(CHUNK_AT[c] + UNIT_AT[n] + 1, c, n) for c in range(2) for n in range(5)] +
                               [(ATTEND_AT[0] + 1, 0, None)], key=lambda step: step[:2])
                for at, c, n in steps:
                    yield at
                    if n is None:
                        gate(row, 0)
                    else:
                        take_unit(row, c, n)

            def linear(row):
                for c in range(1, NT):
                    if c >= 2:
                        yield from chunk(row, c)
                    yield ATTEND_AT[c] + 1
                    gate(row, c)
                yield LN_ATTN_AT
                dve.wait_ge(attn_transposed, row + 1)
                yield from layer_norm(row, LN_ATTN, tiles(6), 4 * EPS, None, 0)
                yield X1_AT
                dve.wait_ge(out_mm, row + 1)
                dve.wait_ge(mod_landed, 16 * row + 16)
                step(V.tensor_tensor(x1_gated, tiles(6), mod_bc[:, 0, :].unsqueeze(1).broadcast_to([P, NT, P]), ALU.mult))
                yield X1_AT + 1
                settle()
                if not is_row(row, 0):
                    dve.wait_ge(carried, 2 * row)
                V.tensor_tensor(x1[:, :, :], x1_gated, x[:, :, :], ALU.add).then_inc(x1_ready, 1)
                yield LN_X1_AT
                dve.wait_ge(x1_ready, row + 1)
                yield from layer_norm(row, LN_X1, x1, EPS, None, 0)
                yield LN_H_AT
                dve.wait_ge(h_ready, row + 1)
                yield from layer_norm(row, LN_H, h, EPS, None, 0)

            def keys(row, core):
                for r in range(2 * HG):
                    yield KEY_AT[r] + 2
                    if core is not None and r % 2 == 0:
                        dve.wait_ge(s2_mm, core * NQ + 16 * (r // 2 + 1))
                    dve.wait_ge(rounded_ready, row * 2 * HG + r + 1)
                    V.scalar_tensor_tensor(kq_parts[:, r, :], bank[:, key_bank(r), :],
                                           const(("k_sel", "q_sel")[r % 2])[:, 1:2],
                                           rounded[:, r % 2, :].bitcast(F32), ALU.mult, ALU.add)\
                        .then_inc(parts_ready, 1)

            def divide(row, g, b):
                heads = slice(g * HJ, (g + 1) * HJ)
                dve.wait_ge(y_transposed, row * HG + g + 1)
                sums = bank[:, b, :].rearrange("p (t h r) -> p t h r", h=HJ, r=QR)
                step(V.reciprocal(recip[:, :, heads], sums[:, :, :, HD]))
                settle()
                V.tensor_tensor(y[:, :, :].rearrange("p t (h d) -> p t h d", d=HD)[:, :, heads], sums[:, :, :, 0:HD],
                                recip[:, :, heads].unsqueeze(3).broadcast_to([P, NT, HJ, HD]), ALU.mult)\
                    .then_inc(y_ready, 1)

            def outputs(row):
                for g in range(HG - 1):
                    yield Y_AT + 16 * g + 1
                    divide(row, g, 5)

            def finish(row):
                yield HEAD + 1
                divide(row, HG - 1, 4)
                yield PROJ_AT + 1
                dve.wait_ge(proj_mm, row + 1)
                dve.wait_ge(carried, 2 * row + 2)
                V.tensor_tensor(h_kept[:, :, :], tiles(4), h_kept[:, :, :], ALU.add).then_inc(x2_ready, 1)
                yield LN2_AT
                dve.wait_ge(x2_ready, row + 1)
                yield from variances(LN2_AT, h_kept, EPS, var2_ready)
                yield LN2_AT + LN_SLOTS
                dve.wait_ge(gb_landed, 16 * row + 16)
                yield from normalize(LN2_AT + LN_SLOTS, h_kept, rstd2_ready, row + 1, norm2_ready, rows)
                V.tensor_copy(rows[:, :, TOKEN].rearrange("p t n -> p (t n)").bitcast(U32),
                              const("tokens")[:, bass.ds(row * NT, NT)])
                yield ROUTE_AT
                dve.wait_ge(logits_mm, row + 1)
                step(V.tensor_tensor(logits[:, :, :], bank[:, 4, 0:NT * E].rearrange("p (t e) -> p t e", e=E),
                                     router_b[:, :].unsqueeze(1).broadcast_to([P, NT, E]), ALU.add))
                yield ROUTE_AT + 1
                settle()
                step(V.tensor_reduce(best[:, :], logits[:, :, :], AX, ALU.max))
                best_bc = best[:, :].unsqueeze(2).broadcast_to([P, NT, E])
                rank_bc = const("rank").unsqueeze(1).broadcast_to([P, NT, E])
                settle()
                step(V.tensor_tensor(onehot[:, :, :], logits[:, :, :], best_bc, ALU.is_equal))
                yield ROUTE_AT + 2
                settle()
                step(V.tensor_tensor(onehot[:, :, :], onehot[:, :, :], rank_bc, ALU.mult))
                settle()
                step(V.tensor_reduce(best[:, :], onehot[:, :, :], AX, ALU.min))
                yield ROUTE_AT + 3
                settle()
                V.tensor_tensor(onehot[:, :, :], rank_bc, best_bc, ALU.is_equal).then_inc(routed, 1)
                yield COUNT_AT + 1
                dve.wait_ge(counted, row + 1)
                for t in range(NT):
                    if t == 2:
                        yield COUNT_AT + 2
                    step(V.tensor_tensor(cum[:, t + 1, :], cum[:, t, :], bank[:, 4, 2 * P + t * E:2 * P + (t + 1) * E],
                                         ALU.add))
                    settle()
                V.tensor_tensor(place[:, :, :], cum[:, 0:NT, :],
                                bank[:, 4, P:P + NT * E].rearrange("p (t e) -> p t e", e=E), ALU.add)\
                    .then_inc(counts_taken, 1)
                yield COUNT_AT + 4
                dve.wait_ge(counts_taken, row + 1)
                step(V.tensor_copy(cum[:, 0, :], cum[:, NT, :]))
                step(V.tensor_tensor(place[:, :, :], place[:, :, :], onehot[:, :, :], ALU.mult))
                yield COUNT_AT + 5
                settle()
                step(V.tensor_reduce(slot_f[:, :], place[:, :, :], AX, ALU.add))
                yield COUNT_AT + 6
                settle()
                V.tensor_scalar(slot[:, :], slot_f[:, :], 0.0, float(E * REGION - 1), ALU.max, ALU.min)\
                    .then_inc(slots_ready, 1)

            def split_maxima(i, g):
                dve.wait_ge(max_taken, i * NQ + 16 * (g + 1))
                exact = negmax[:, g].rearrange("p j t -> p t j")
                step(V.tensor_copy(shift[:, g, :, :, 0], exact))
                settle()
                V.tensor_tensor(shift[:, g, :, :, 1], exact, shift[:, g, :, :, 0].bitcast(F32),
                                ALU.subtract).then_inc(shift_ready, 1)

            def softmax_row(i, following, *stages):
                stages = [Stage(steps) for steps in stages]
                for s in range(HEAD, SLOTS):
                    for stage in stages:
                        stage.go_on(s)
                    row, a = max_tile(i, following, s)
                    if row is not None:
                        g, j, t = a // (HJ * NT), a // NT % HJ, a % NT
                        dve.wait_ge(max_mm, row * NQ + a + 1)
                        V.tensor_reduce(negmax[:, g, j, t:t + 1], bank[:, a % 2, :], AX, ALU.max, negate=True)\
                            .then_inc(max_taken, 1)
                        if a % 16 == 15:
                            split_maxima(row, g)
                for stage in stages:
                    stage.go_on(END - 1)

            first_inputs = Stage(inputs(0))
            first_inputs.go_on(T_X_AT)
            dve.wait_ge(loaded, 16 * N_LOADS)
            V.tensor_copy(ident_r[:, :], ident).then_inc(prepared, 1)
            V.tensor_copy(cum[:, 0, :], const("regions")).then_inc(cum_ready, 1)
            dve.wait_ge(zeroed, 3)
            for part in range(2):
                for g in range(HG):
                    src = msa_w[:, part * P + g * QR:part * P + (g + 1) * QR].rearrange("p (j d) -> p j d", d=HD)
                    V.tensor_copy(rep_w[:, part, g, :, 0:3, :], src.unsqueeze(2).broadcast_to([P, HJ, 3, HD]))\
                        .then_inc(prepared, 1)
            dve.wait_ge(gate_w_mm, 1)
            V.tensor_copy(attn_w[:, 3 * P:4 * P], bank[:, 2, 0:P]).then_inc(prepared, 1)
            dve.wait_ge(cum_ready, 1)
            first_inputs.go_on(END - 1)
            softmax_row(None, 0, linear(0), inputs(1), keys(0, None))
            softmax_row(0, 1, linear(1), outputs(0), inputs(2), keys(1, 0))
            so_far = steps[1]
            with dve.Fori(1, B - 2) as i:
                steps[:] = [(i - 1) * DVE_STEPS + so_far, 0]
                softmax_row(i, i + 1, finish(i - 1), linear(i + 1), outputs(i), inputs(i + 2), keys(i + 1, i))
                assert steps[1] == DVE_STEPS, steps
            steps[:] = [(B - 3) * DVE_STEPS + so_far, 0]
            softmax_row(B - 2, B - 1, finish(B - 3), linear(B - 1), outputs(B - 2), keys(B - 1, B - 2))
            softmax_row(B - 1, None, finish(B - 2), outputs(B - 1))
            softmax_row(None, None, finish(B - 1))
            settle()

            count = [0]

            def route(instruction):
                count[0] += 1
                instruction.then_inc(route_step, 1)
                dve.wait_ge(route_step, count[0])

            V.tensor_scalar(pads_at[:, :], cum[:, 0, :], 1.0, None, ALU.add).then_inc(pads_at_ready, 1)
            route(V.tensor_tensor(counts[:, :], cum[:, 0, :], const("regions"), ALU.subtract))
            route(V.tensor_tensor(over[:, :, :], counts[:, :].unsqueeze(2).broadcast_to([P, E, TILES]),
                                  const("tile_starts").unsqueeze(1).broadcast_to([P, E, TILES]), ALU.is_gt))
            route(V.tensor_reduce(tiles_of[:, :], over[:, :, :], AX, ALU.add))
            route(V.tensor_tensor(square[:, :, :], tiles_of[:, :].unsqueeze(1).broadcast_to([P, E, E]),
                                  const("upto").rearrange("p (a b) -> p a b", b=E), ALU.mult))
            route(V.tensor_reduce(ends[:, :], square[:, :, :], AX, ALU.add))
            ends_bc = ends[:, :].unsqueeze(1).broadcast_to([P, SLOT_TILES, E])
            route(V.tensor_tensor(past[:, :, :], const("slot_tiles").unsqueeze(2).broadcast_to([P, SLOT_TILES, E]),
                                  ends_bc, ALU.is_ge))
            V.tensor_reduce(expert_f[:, :], past[:, :, :], AX, ALU.add).then_inc(route_step, 1)
            count[0] += 1
            route(V.tensor_tensor(past_ends[:, :, :], past[:, :, :], ends_bc, ALU.mult))
            V.tensor_scalar(region[:, :], expert_f[:, :], float(REGION), None, ALU.mult).then_inc(route_step, 1)
            count[0] += 1
            route(V.tensor_reduce(first[:, :], past_ends[:, :, :], AX, ALU.max))
            route(V.tensor_tensor(first[:, :], const("slot_tiles"), first[:, :], ALU.subtract))
            route(V.scalar_tensor_tensor(region[:, :], first[:, :], float(P), region[:, :], ALU.mult, ALU.add))
            V.tensor_scalar(tile_at[:, :], region[:, :], float(E * REGION), None, ALU.min).then_inc(experts_ready, 1)
            V.tensor_scalar(expert[:, :], expert_f[:, :], float(E - 1), None, ALU.min).then_inc(experts_ready, 1)

            def copy_w1(n, r, is_first):
                e = dve.value_load(expert[0:1, bass.ds(n, 1)], min_val=0, max_val=E - 1)
                if not is_first:
                    dve.wait_ge(up_mm, n - 1)
                V.tensor_copy(w1_tile[:, r % 2, :], w1[:, bass.ds(e, 1), :].rearrange("p a n -> p (a n)"))                    .then_inc(w1_copied, 1)

            def gate_y(k, r, is_first):
                n = k * RING + r
                dve.wait_ge(down_mm, n + 1)
                if r >= 4:
                    dve.wait_ge(out_stored[r - 4], 16 * (k + 1))
                elif not is_first:
                    dve.wait_ge(out_stored[r + 4], 16 * k)
                V.tensor_tensor(y_tile[:, r % 4, :], bank[:, 6 + r % 2, 0:P], z_in[:, r, GATE], ALU.mult)\
                    .then_inc(y_scaled, 1)
                dve.wait_ge(y_scaled, n + 1)
                V.tensor_tensor(y_tile[:, r % 4, :], y_tile[:, r % 4, :], z_in[:, r, RESIDUAL], ALU.add)\
                    .then_inc(y_done, 1)

            dve.wait_ge(experts_ready, 2)
            dve.wait_ge(w_loaded, 32)
            copy_w1(0, 0, True)
            copy_w1(1, 1, True)
            for r in range(RING):
                copy_w1(r + 2, r, False)
                gate_y(0, r, True)
            with dve.Fori(1, SLOT_TILES // RING - 1) as k:
                for r in range(RING):
                    copy_w1(k * RING + r + 2, r, False)
                    gate_y(k, r, False)
            for r in range(RING):
                n = SLOT_TILES - RING + r
                if n + 2 < SLOT_TILES:
                    copy_w1(n + 2, r, False)
                gate_y(SLOT_TILES // RING - 1, r, False)

def kernel(**inputs):
    import concourse.bacc as bacc
    from concourse.bass_utils import run_bass_kernel_spmd

    g = {k: np.ascontiguousarray(v) for k, v in inputs.items()}
    x = g["L0_attn_x"]
    arrays = {"x": x, "table": constants(x.shape[1]), "cT": np.ascontiguousarray(g["L0_c"].T), "wmod": g["L0_wmod"],
              "ln_cols": np.ascontiguousarray(np.stack([g[k] for k in (
                  "L0_attn_ln_w", "L0_attn_ln_b", "L0_ffn_ln1_w", "L0_ffn_ln1_b", "L0_ffn_ln2_w",
                  "L0_ffn_ln2_b")], axis=1))}
    for k in ("Wq", "Wk", "Wv", "Wo", "Wg2"):
        arrays[k] = g["L0_attn_" + k]
    arrays["Wg1T"] = np.ascontiguousarray(g["L0_attn_Wg1"].T)
    for k in ("w_qkv", "w_proj", "gate_w", "gate_b", "w1", "w2"):
        arrays[k] = g["L0_ffn_" + k]
    nc = bacc.Bacc("TRN2", target_bir_lowering=False, num_devices=1)
    aps = {k: nc.dram_tensor("in_" + k, v.shape, F32, kind="ExternalInput").ap() for k, v in arrays.items()}
    out = nc.dram_tensor("out_0", x.shape, F32, kind="ExternalOutput").ap()
    scratch = nc.dram_tensor("modulation", (x.shape[0], 6 * P), F32).ap()
    slots = nc.dram_tensor("slots", (E * REGION + P, SLOT), F32).ap()
    build(nc, aps, out, scratch, slots)
    r = run_bass_kernel_spmd(nc, [{"in_" + k: v for k, v in arrays.items()}], core_ids=[0])
    return r.results[0]["out_0"]
```
